# Optimizing a Trainium2 kernel written in Bass

```python
import numpy as np
import jax
import jax.numpy as jnp

def _softmax(x, axis=-1):
    return jax.nn.softmax(x, axis=axis)

def _gelu(x):
    return jax.nn.gelu(x, approximate=True)

def _silu(x):
    return jax.nn.silu(x)

def _sigmoid(x):
    return jax.nn.sigmoid(x)

def _layernorm(x, axis=-1, eps=1e-05):
    m = jnp.mean(x, axis=axis, keepdims=True)
    v = jnp.var(x, axis=axis, keepdims=True)
    return (x - m) / jnp.sqrt(v + eps)

def _scatter_add(tgt, idx, src, axis=0):
    return tgt.at[idx].add(src)

def _segment_sum(src, seg, n):
    return jax.ops.segment_sum(src, seg, n)
kernel_name = 'mk_seq_postln_d1_jaxref_r4_1cc643'

def setup_inputs(seed: int=0):
    np.random.seed(seed)
    _w = jnp.asarray

    def _L0_attn_setup():
        import jax, jax.numpy as jnp
        import numpy as np
        B, T, C = (4, 512, 256)
        H = 16
        D = C // H
        key = jax.random.key(seed)
        k1, k2, k3, k4, k5 = jax.random.split(key, 5)
        s = 0.02
        return {'x': jax.random.normal(k1, (B, T, C), dtype=jnp.float32), 'Wqkv': jax.random.normal(k2, (C, 3 * C), dtype=jnp.float32) * s, 'bqkv': jnp.zeros((3 * C,), dtype=jnp.float32), 'Wout': jax.random.normal(k3, (C, C), dtype=jnp.float32) * s, 'bout': jnp.zeros((C,), dtype=jnp.float32)}
    _L0_attn_in = _L0_attn_setup()

    def _L0_ffn_setup():
        import jax, jax.numpy as jnp
        import numpy as np
        D_IN, D_HID = (256, 1024)

        def _ternary(key, shape):
            return jax.random.randint(key, shape, -1, 2).astype(jnp.float32)

        def _tlin(x, w, s):
            return jnp.einsum('bsi,oi->bso', x, w) * s
        key = jax.random.key(seed)
        ks = jax.random.split(key, 12)
        inv = lambda fan: 1.0 / np.sqrt(fan).astype(np.float32)
        return {'x': jax.random.normal(ks[0], (4, 512, D_IN), dtype=jnp.float32), 'w1_w': _ternary(ks[1], (D_HID, D_IN)), 'w1_s': jax.random.uniform(ks[2], (D_HID,), dtype=jnp.float32) * inv(D_IN), 'w2_w': _ternary(ks[3], (D_HID, D_IN)), 'w2_s': jax.random.uniform(ks[4], (D_HID,), dtype=jnp.float32) * inv(D_IN), 'h1_w': _ternary(ks[5], (D_HID, D_HID)), 'h1_s': jax.random.uniform(ks[6], (D_HID,), dtype=jnp.float32) * inv(D_HID), 'h2_w': _ternary(ks[7], (D_HID, D_HID)), 'h2_s': jax.random.uniform(ks[8], (D_HID,), dtype=jnp.float32) * inv(D_HID), 'w3_w': _ternary(ks[9], (D_IN, D_HID)), 'w3_s': jax.random.uniform(ks[10], (D_IN,), dtype=jnp.float32) * inv(D_HID)}
    _L0_ffn_in = _L0_ffn_setup()
    _d = {'L0_attn_x': _L0_attn_in['x'], 'L0_attn_Wqkv': _L0_attn_in['Wqkv'], 'L0_attn_bqkv': _L0_attn_in['bqkv'], 'L0_attn_Wout': _L0_attn_in['Wout'], 'L0_attn_bout': _L0_attn_in['bout'], 'L0_ffn_w1_w': _L0_ffn_in['w1_w'], 'L0_ffn_w1_s': _L0_ffn_in['w1_s'], 'L0_ffn_w2_w': _L0_ffn_in['w2_w'], 'L0_ffn_w2_s': _L0_ffn_in['w2_s'], 'L0_ffn_h1_w': _L0_ffn_in['h1_w'], 'L0_ffn_h1_s': _L0_ffn_in['h1_s'], 'L0_ffn_h2_w': _L0_ffn_in['h2_w'], 'L0_ffn_h2_s': _L0_ffn_in['h2_s'], 'L0_ffn_w3_w': _L0_ffn_in['w3_w'], 'L0_ffn_w3_s': _L0_ffn_in['w3_s']}
    _x0 = _d['L0_attn_x']
    _d['L0_attn_x'] = jax.random.normal(jax.random.fold_in(jax.random.key(seed), 1), (16, 512, 256), dtype=_x0.dtype)
    del _x0
    return _d

def reference(L0_attn_x, L0_attn_Wqkv, L0_attn_bqkv, L0_attn_Wout, L0_attn_bout, L0_ffn_w1_w, L0_ffn_w1_s, L0_ffn_w2_w, L0_ffn_w2_s, L0_ffn_h1_w, L0_ffn_h1_s, L0_ffn_h2_w, L0_ffn_h2_s, L0_ffn_w3_w, L0_ffn_w3_s):

    def _L0_attn_ref(x, Wqkv, bqkv, Wout, bout):
        import jax, jax.numpy as jnp
        import numpy as np
        B, T, C = (4, 512, 256)
        H = 16
        D = C // H
        b, t, c = x.shape
        scale = D ** (-0.5)
        qkv = x @ Wqkv + bqkv
        qkv = qkv.reshape(b, t, 3, H, D)
        q = qkv[:, :, 0].transpose(0, 2, 1, 3)
        k = qkv[:, :, 1].transpose(0, 2, 1, 3)
        v = qkv[:, :, 2].transpose(0, 2, 1, 3)
        att = jnp.einsum('bhqd,bhkd->bhqk', q, k) * scale
        causal = jnp.tril(jnp.ones((t, t), dtype=bool))
        att = jnp.where(causal, att, -jnp.inf)
        att = jax.nn.softmax(att, axis=-1)
        y = jnp.einsum('bhqk,bhkd->bhqd', att, v)
        y = y.transpose(0, 2, 1, 3).reshape(b, t, c)
        return y @ Wout + bout

    def _L0_ffn_ref(x, w1_w, w1_s, w2_w, w2_s, h1_w, h1_s, h2_w, h2_s, w3_w, w3_s):
        import jax, jax.numpy as jnp
        import numpy as np
        D_IN, D_HID = (256, 1024)

        def _ternary(key, shape):
            return jax.random.randint(key, shape, -1, 2).astype(jnp.float32)

        def _tlin(x, w, s):
            return jnp.einsum('bsi,oi->bso', x, w) * s
        h = jax.nn.silu(_tlin(x, w1_w, w1_s)) * _tlin(x, w2_w, w2_s)
        h = jax.nn.gelu(_tlin(h, h1_w, h1_s), approximate=False)
        h = jax.nn.gelu(_tlin(h, h2_w, h2_s), approximate=False)
        return _tlin(h, w3_w, w3_s)
    x = L0_attn_x
    x = _layernorm(x + _L0_attn_ref(x, L0_attn_Wqkv, L0_attn_bqkv, L0_attn_Wout, L0_attn_bout), axis=-1)
    x = _layernorm(x + _L0_ffn_ref(x, L0_ffn_w1_w, L0_ffn_w1_s, L0_ffn_w2_w, L0_ffn_w2_s, L0_ffn_h1_w, L0_ffn_h1_s, L0_ffn_h2_w, L0_ffn_h2_s, L0_ffn_w3_w, L0_ffn_w3_s), axis=-1)
    return x

_drawn_inputs = setup_inputs


def setup_inputs(seed=0):
    import zlib

    import numpy as np

    out = dict(_drawn_inputs(seed))
    spreads = {'L0_attn_bqkv': (0.0, 0.1), 'L0_attn_bout': (0.0, 0.1)}
    factors = {'L0_attn_Wqkv': 4.786,
     'L0_ffn_w1_w': 8.0,
     'L0_ffn_w1_s': 8.0,
     'L0_ffn_w2_w': 8.0,
     'L0_ffn_w2_s': 8.0,
     'L0_ffn_h1_w': 8.0,
     'L0_ffn_h1_s': 8.0,
     'L0_ffn_h2_w': 8.0,
     'L0_ffn_h2_s': 8.0,
     'L0_ffn_w3_w': 8.0,
     'L0_ffn_w3_s': 8.0}
    for name, (base, spread) in spreads.items():
        noise = np.random.default_rng([zlib.crc32(name.encode()), seed]).standard_normal(out[name].shape)
        drawn = base * np.exp(spread * noise) if base else spread * noise
        out[name] = jnp.asarray(drawn.astype(out[name].dtype))
    for name, factor in factors.items():
        out[name] = (out[name] * factor).astype(out[name].dtype)
    return out
```

```python
from contextlib import ExitStack

import numpy as np

import concourse.bass as bass
from concourse import mybir

F32 = mybir.dt.float32
F32R = mybir.dt.float32r
BF16 = mybir.dt.bfloat16
I32 = mybir.dt.int32
ACT = mybir.ActivationFunctionType
ALU = mybir.AluOpType
AX_X = mybir.AxisListType.X

P = 128
B, T, C = 16, 512, 256
H = 16
D = C // H
HID = 1024
SCALE = float(D) ** -0.5
EPS = 1e-5
NEG = -3.0e38
LOW_BITS = 0xFFF

CB = C // P
KB = HID // P
TB = T // P
HALF = T // 2
G = 4
NG = H // G
PAIRS = G // 2
SROWS = 3 * D
EROWS = SROWS + 2
VW = D + 1
NP_BUF = 4
MISC = 3


def plan_iteration():
    steps = []

    def add(kind, off, *args):
        steps.append((kind, off, args))

    late_hi = []
    for g in range(NG):
        maxes = [(g + 1, t, p) for t in reversed(range(TB)) for p in range(PAIRS)] if g + 1 < NG else []
        for kt in range(TB):
            for p in range(PAIRS):
                add("exp", 0, g, kt, p)
                for _ in range([2, 1, 1, 0][kt] if p == 0 else [1, 2, 1, 0][kt]):
                    if maxes:
                        add("max", 0, *maxes.pop(0))
            if late_hi:
                add("ffn_hi", -1, late_hi.pop(0))
            if kt:
                add("pv", 0, g, kt - 1)
        if g + 1 < NG:
            add("neg_max", 0, g + 1)
        if g == 0:
            for c in range(CB):
                add("x1_turn", -1, c)
        add("gate", -1, 2 * g)
        add("up", -1, 2 * g)
        add("gate", -1, 2 * g + 1)
        add("pv", 0, g, TB - 1)
        add("o_out", 0, g)
        add("up", -1, 2 * g + 1)
        late_hi = [2 * g, 2 * g + 1]
        if g + 2 < NG:
            add("stack", 0, g + 2)
        if g == 2:
            add("load_x", 0)
            add("load_xT", 1)
    for j in late_hi:
        add("ffn_hi", -1, j)
    add("den", 0)
    extras = {
        1: [("qk", 1, (0,))], 2: [("v", 1, (0,))], 3: [("v", 1, (1,))], 4: [("v", 1, (2,))],
        5: [("qk", 1, (1,)), ("stack", 1, (0,))], 6: [("v", 1, (3,))],
        8: [("den_turn", 0, ())], 9: [("qk", 1, (2,)), ("stack", 1, (1,))],
        10: [("y", 0, (0,))], 11: [("y", 0, (1,))], 12: [("ln1_stats", 0, ())], 13: [("qk", 1, (3,))],
        17: [("ffn_out", -1, (0,))], 19: [("ln2", -1, (0,))],
        20: [("max", 1, (0, 3, 0))], 21: [("max", 1, (0, 3, 1))], 22: [("max", 1, (0, 2, 0))],
        23: [("max", 1, (0, 2, 1))], 24: [("max", 1, (0, 1, 0))], 25: [("max", 1, (0, 1, 1))],
        26: [("max", 1, (0, 0, 0))], 27: [("max", 1, (0, 0, 1))], 29: [("neg_max", 1, (0,))],
    }
    u = 0
    for half in range(2):
        for layer in ("h1", "h2"):
            for j in range(KB):
                add(layer, -1, half, j)
                steps.extend(extras.get(u, []))
                u += 1
    add("ffn_out", -1, 1)
    add("ln1", 0)
    add("ln2", -1, 1)
    return steps


STEPS = plan_iteration()
BANKED = [s for s in STEPS if s[0] in
          ("qk", "v", "gate", "up", "h1", "h2", "ffn_out", "y", "x1_turn", "neg_max")]


def ring_banks():
    at, banks = 0, {}
    for kind, off, args in STEPS:
        n = 2 if kind == "den_turn" else 1 if (kind, off, args) in BANKED else 0
        for m in range(n):
            key = (kind, off, args + (m,)) if kind == "den_turn" else (kind, off, args)
            banks[key] = at % MISC
            at += 1
    return banks


BANKS = ring_banks()


def steps_of(i):
    return [s for s in STEPS if i is None or 0 <= i + s[1] < B]


def over(nc, base, name, shape, dt):
    return nc.alloc_sbuf_tensor_at(name, shape, dt, offset=base)


def build(nc, x, xT, w_qk, w_v, w_out, w_ffn, cols_in, b_out, s3, out):
    with ExitStack() as ctx:
        def sb(name, shape, dt=F32):
            return ctx.enter_context(nc.sbuf_tensor(name, shape, dt))

        def psum(name, shape):
            return ctx.enter_context(nc.psum_tensor(name, shape, F32))

        def sem(name):
            return ctx.enter_context(nc.semaphore(name))

        def dram(name, shape):
            return nc.dram_tensor(name, shape, F32, kind="Internal").ap()

        W1 = sb("W1", [P, CB, HID], F32R)
        W2 = sb("W2", [P, CB, HID], F32R)
        H1 = sb("H1", [P, KB, HID], F32R)
        H2 = sb("H2", [P, KB, HID], F32R)
        W3 = sb("W3", [P, KB, C], F32R)
        FFN = (W1, W2, H1, H2, W3)
        Wqk = sb("Wqk", [P, CB, NG, P])
        Wv = sb("Wv", [P, CB, C])
        Wout = sb("Wout", [P, CB, C])
        Qs = sb("Qs", [P, 2, PAIRS, T], F32R)
        Ks = sb("Ks", [P, 2, PAIRS, T], F32R)
        Vo = sb("Vo", [P, TB, H, VW])
        Osb = sb("Osb", [P, T])
        Oc = sb("Oc", [P, CB, T])
        low_at = nc.sbuf_base
        Xhi = sb("Xhi", [P, KB, T], F32R)
        low = over(nc, low_at, "low_bits", [P, KB * T], I32)
        Xlo = sb("Xlo", [P, KB, T], F32R)
        x1Thi = sb("x1Thi", [P, CB, T], F32R)
        x1Tlo = sb("x1Tlo", [P, CB, T], F32R)
        full = sb("full", [P, 2, T])
        xr = sb("xr", [P, TB, C])
        x1 = sb("x1", [P, TB, C])
        z = sb("z", [P, 2, C])
        py_at = nc.sbuf_base
        probs = sb("probs", [P, NP_BUF, 2, T])
        Yhi = over(nc, py_at, "Yhi", [P, KB, HALF], F32R)
        Ylo = over(nc, py_at + KB * HALF * 4, "Ylo", [P, KB, HALF], F32R)
        ct_at = nc.sbuf_base
        c_hi = sb("c_hi", [P, T], F32R)
        c_lo = sb("c_lo", [P, T], F32R)
        th = over(nc, ct_at, "th", [P, T], F32)
        xn_at = nc.sbuf_base
        xTs = sb("xTs", [P, CB, T])
        nm_hi = over(nc, xn_at, "nm_hi", [G, T], F32R)
        nm_lo = over(nc, xn_at + T * 4, "nm_lo", [G, T], F32R)
        mask = sb("mask", [P, T], BF16)
        ident = sb("ident", [P, P])
        sel = sb("sel", [H, CB, P])
        b_tot = sb("b_tot", [P, C])
        s3b = sb("s3b", [P, C])
        cols = sb("cols", [P, 40])
        bqk_c, bv_c = cols[:, 0:NG], cols[:, 4:6]
        s1_c, s2_c, sh1_c, sh2_c = (cols[:, 8 * n:8 * n + 8] for n in (1, 2, 3, 4))
        mx = sb("mx", [P, TB, G])
        dn = sb("dn", [P, H * T // P])
        rc = sb("rc", [P, H * T // P])
        st1, mv1, rs1 = sb("st1", [P, TB, 6]), sb("mv1", [P, TB, 2]), sb("rs1", [P, TB])
        st2, mv2, rs2 = sb("st2", [P, 2, 6]), sb("mv2", [P, 2, 2]), sb("rs2", [P, 2])
        minus_half = sb("minus_half", [P, TB])
        lowmax = sb("lowmax", [P, 16])
        ones_c = sb("ones_c", [P, 1])
        flag = sb("flag", [1, 1], I32)

        pS = psum("pS", [P, 2, T])
        pM = psum("pM", [P, 2, T])
        pO = psum("pO", [P, T])
        ring = psum("ring", [P, MISC, T])

        raw = [dram(f"raw{n}", w.shape) for n, w in enumerate(w_ffn)]
        qk_d = dram("qk_d", [2, NG, P, T])
        nm_d = dram("nm_d", [2, G, T])
        den_d = dram("den_d", [H, T])
        rec_d = dram("rec_d", [H, T])

        xT_in, x_in, params_in, raw_in, weights_in = map(sem, ("xT_in", "x_in", "params_in", "raw_in", "weights_in"))
        qk_saved, nm_saved, nm_in, o_moved = map(sem, ("qk_saved", "nm_saved", "nm_in", "o_moved"))
        stack_in = [sem("stack_in0"), sem("stack_in1")]
        den_in, rec_saved, rec_in, stored = map(sem, ("den_in", "rec_saved", "rec_in", "stored"))
        qk_ready, v_ready, e_ready, m_ready, pv_done = map(sem, ("qk_ready", "v_ready", "e_ready", "m_ready", "pv_done"))
        nt_ready, xt_ready, g_ready, u_ready, h_ready = map(sem, ("nt_ready", "xt_ready", "g_ready", "u_ready", "h_ready"))
        f_ready, y_ready, r_ready = map(sem, ("f_ready", "y_ready", "r_ready"))
        qk_hi, exp_done, tanh_done, x_hi, h_full = map(sem, ("qk_hi", "exp_done", "tanh_done", "x_hi", "h_full"))
        o_out, nm_hi_done, x1_hi, v_copied = map(sem, ("o_out", "nm_hi_done", "x1_hi", "v_copied"))
        qk_lo, m_done, nm_lo_done, gated, ffn_full, h_lo = map(sem, ("qk_lo", "m_done", "nm_lo_done", "gated", "ffn_full", "h_lo"))
        x1_lo, rc_done, o_norm, ln1, ln2 = map(sem, ("x1_lo", "rc_done", "o_norm", "ln1", "ln2"))
        mask_done, x_lo, xr_ready, ln1_pow, ln2_pow = map(sem, ("mask_done", "x_lo", "xr_ready", "ln1_pow", "ln2_pow"))
        consts, setup_v, setup_t, passed = map(sem, ("consts", "setup_v", "setup_t", "passed"))

        LN1, LN2 = 7, 12
        N_PARAMS = 6
        N_CONSTS = 10

        def need(eng, s, n):
            if not (isinstance(n, int) and n <= 0):
                eng.wait_ge(s, n)

        def held(eng):
            eng.sem_inc(passed, 1)

        def pipeline(eng, body):
            for i in (-1, 0, 1, 2):
                body(i, steps_of(i))
            with eng.Fori(3, B - 1) as i:
                body(i, steps_of(None))
            for i in (B - 1, B):
                body(i, steps_of(i))

        def e_of(g, kt, p):
            return (g * TB + kt) * PAIRS + p

        def u_of(kind, half, j):
            return (2 * half + (kind == "h2")) * KB + j

        def e_cols(kt):
            return T - kt * P

        def m_cols(t):
            return (t + 1) * P

        block = ctx.enter_context(nc.Block())

        @block.sync
        def _(sp):
            sp.dma_start(Wqk[:], w_qk.rearrange("(c p) g n -> p c g n", p=P)).then_inc(params_in, 16)
            sp.dma_start(cols[:], cols_in).then_inc(params_in, 16)
            sp.dma_start(xTs[:], xT[0].rearrange("(c p) t -> p c t", p=P)).then_inc(xT_in, 16)
            sp.dma_start(Wv[:], w_v.rearrange("(c p) n -> p c n", p=P)).then_inc(params_in, 16)
            sp.dma_start(Wout[:], w_out.rearrange("(c p) n -> p c n", p=P)).then_inc(params_in, 16)
            sp.dma_start(b_tot[:], b_out.rearrange("(a n) -> a n", a=1).broadcast_to([P, C])).then_inc(params_in, 16)
            sp.dma_start(s3b[:], s3.rearrange("(a n) -> a n", a=1).broadcast_to([P, C])).then_inc(params_in, 16)

            def move(i, steps):
                for kind, off, a in steps:
                    b = i + off
                    if kind == "load_xT" and not (isinstance(b, int) and b == 0):
                        sp.wait_ge(v_ready, b * TB)
                        held(sp)
                        sp.wait_ge(nm_saved, b * (NG * 32))
                        held(sp)
                        sp.dma_start(xTs[:], xT[bass.ds(b, 1)].rearrange("a (c p) t -> p (a c) t", p=P)).then_inc(xT_in, 16)
                    elif kind == "load_x":
                        need(sp, ln1, b * LN1)
                        held(sp)
                        sp.dma_start(xr[:], x[bass.ds(b, 1)].rearrange("a (t p) c -> p (a t) c", p=P)).then_inc(x_in, 16)
                    elif kind == "qk":
                        g, = a
                        sp.wait_ge(qk_lo, b * NG + g + 1)
                        sp.dma_start(qk_d[0, g], c_hi[:].bitcast(F32)).then_inc(qk_saved, 16)
                        sp.dma_start(qk_d[1, g], c_lo[:].bitcast(F32)).then_inc(qk_saved, 16)
                    elif kind == "stack":
                        g, = a
                        slot = g % 2
                        sp.wait_ge(qk_saved, (b * NG + g + 1) * 32)
                        held(sp)
                        need(sp, e_ready, b * (NG * TB * PAIRS) + (g - 1) * TB * PAIRS)
                        if g == 0 and isinstance(b, int) and b == 0:
                            sp.wait_ge(consts, N_CONSTS)
                        if g == 1 and isinstance(b, int) and b == 0:
                            sp.wait_ge(consts, N_CONSTS)
                        for dst, qk, parts in ((Qs, 0, (0, 1, 0)), (Ks, 1, (0, 0, 1))):
                            for s in range(2):
                                for r, part in enumerate(parts):
                                    rows = qk_d[part, g, qk * G * D:(qk + 1) * G * D].rearrange(
                                        "(p s d) n -> s d p n", p=PAIRS, s=2)[s]
                                    at = 64 * s + r * D
                                    sp.dma_start(dst[at:at + D, slot].bitcast(F32), rows).then_inc(stack_in[slot], 16)
                    elif kind == "neg_max":
                        g, = a
                        sp.wait_ge(nm_lo_done, b * NG + g + 1)
                        sp.dma_start(nm_d[0], nm_hi[:].bitcast(F32)).then_inc(nm_saved, 16)
                        sp.dma_start(nm_d[1], nm_lo[:].bitcast(F32)).then_inc(nm_saved, 16)
                        sp.wait_ge(nm_saved, (b * NG + g + 1) * 32)
                        for s in range(2):
                            at = 64 * s + SROWS
                            sp.dma_start(Qs[at:at + 2, g % 2].bitcast(F32),
                                         nm_d.rearrange("h (p s) n -> s h p n", s=2)[s]).then_inc(nm_in, 16)
                    elif kind == "o_out":
                        g, = a
                        sp.wait_ge(o_out, b * NG + g + 1)
                        held(sp)
                        if g == 0:
                            need(sp, y_ready, b * 2)
                        held(sp)
                        for j in range(G):
                            at = 64 * (g % 2) + D * j
                            sp.dma_start(Oc[at:at + D, g // 2], Osb[32 * j:32 * j + D]).then_inc(o_moved, 16)
                        sp.dma_start(den_d[g * G:(g + 1) * G], Osb[D:P:32, :]).then_inc(o_moved, 16)
                    elif kind == "den":
                        sp.wait_ge(o_moved, (b + 1) * (NG * 80))
                        sp.dma_start(dn[:], den_d.rearrange("h (c n) -> (h c) n", n=H * T // P)).then_inc(den_in, 16)
                        sp.wait_ge(rc_done, b + 1)
                        sp.dma_start(rec_d.rearrange("h (c n) -> (h c) n", n=H * T // P), rc[:]).then_inc(rec_saved, 16)
                        sp.wait_ge(rec_saved, (b + 1) * 16)
                        sp.dma_start(Osb[0:H], rec_d).then_inc(rec_in, 16)
                    elif kind == "ln2":
                        half, = a
                        sp.wait_ge(ln2, b * LN2 + 6 * half + 6)
                        held(sp)
                        sp.dma_start(out[bass.ds(b, 1)].rearrange("a (t p) c -> p (a t) c", p=P)[:, 2 * half:2 * half + 2],
                                     z[:]).then_inc(stored, 16)

            for i in (-1, 0, 1, 2):
                move(i, steps_of(i))
                if i == -1:
                    sp.wait_ge(raw_in, 16 * len(FFN))
                    for w, r in zip(FFN, raw):
                        sp.dma_start(w[:].bitcast(F32), r.rearrange("(k p) n -> p k n", p=P)).then_inc(weights_in, 16)
            with sp.Fori(3, B - 1) as i:
                move(i, steps_of(None))
            for i in (B - 1, B):
                move(i, steps_of(i))
            sp.wait_ge(stored, B * 32)

        @block.gpsimd
        def _(pool):
            nc.gpsimd.memset(ident[:], 0.0).then_inc(consts, 1)
            nc.gpsimd.memset(mask[:], 0.0).then_inc(consts, 1)
            nc.gpsimd.memset(sel[:], 1.0).then_inc(consts, 1)
            nc.gpsimd.memset(minus_half[:], -0.5).then_inc(consts, 1)
            nc.gpsimd.memset(ones_c[:], 1.0).then_inc(consts, 1)
            nc.gpsimd.memset(Vo[:], 1.0).then_inc(consts, 1)
            pool.wait_ge(consts, 6)
            nc.gpsimd.affine_select(out=ident[:], in_=ident[:], compare_op=ALU.not_equal, fill=1.0, base=0,
                                    pattern=[[-1, P]], channel_multiplier=1).then_inc(consts, 1)
            tri = mask[:, T - P:T]
            nc.gpsimd.affine_select(out=tri, in_=tri, compare_op=ALU.is_ge, fill=NEG, base=0,
                                    pattern=[[-1, P]], channel_multiplier=1).then_inc(consts, 1)
            heads = sel[:].rearrange("h c (e d) -> h (c e) d", d=D)
            nc.gpsimd.affine_select(out=heads, in_=heads, compare_op=ALU.is_equal, fill=0.0, base=0,
                                    pattern=[[-1, H], [0, D]], channel_multiplier=1).then_inc(consts, 1)
            nc.gpsimd.memset(Ks[:].bitcast(F32), 1.0).then_inc(consts, 1)

            def work(i, steps):
                for kind, off, a in steps:
                    b = i + off
                    if kind == "exp":
                        g, kt, p = a
                        e = e_of(g, kt, p)
                        pool.wait_ge(exp_done, b * (NG * TB * PAIRS) + e + 1)
                        held(pool)
                        tri_p = probs[:, e % NP_BUF, :, 0:P]
                        nc.gpsimd.affine_select(out=tri_p, in_=tri_p, compare_op=ALU.is_ge, fill=0.0, base=0,
                                                pattern=[[0, 2], [1, P]], channel_multiplier=-1).then_inc(mask_done, 1)
                    elif kind == "ffn_hi":
                        j, = a
                        pool.wait_ge(x_hi, b * KB + j + 1)
                        nc.gpsimd.tensor_tensor(Xlo[:, j], full[:, j % 2], Xhi[:, j].bitcast(F32),
                                                ALU.subtract).then_inc(x_lo, 1)
                    elif kind == "load_x":
                        if isinstance(b, int) and b == 0:
                            pool.wait_ge(setup_v, 4)
                        pool.wait_ge(x_in, (b + 1) * 16)
                        for t in range(TB):
                            add_b = nc.gpsimd.tensor_tensor(xr[:, t], xr[:, t], b_tot[:], ALU.add)
                        add_b.then_inc(xr_ready, 1)
                    elif kind == "ln1_stats":
                        pool.wait_ge(ln1, b * LN1 + 6)
                        nc.gpsimd.tensor_tensor(rs1[:], rs1[:], minus_half[:], ALU.pow).then_inc(ln1_pow, 1)
                    elif kind == "ln2":
                        half, = a
                        pool.wait_ge(ln2, b * LN2 + 6 * half + 5)
                        nc.gpsimd.tensor_tensor(rs2[:], rs2[:], minus_half[:, 0:2], ALU.pow).then_inc(ln2_pow, 1)

            pipeline(pool, work)

        @block.scalar
        def _(act):
            for w, r in zip(w_ffn, raw):
                act.dma_start(r, w).then_inc(raw_in, 16)

            def work(i, steps):
                for kind, off, a in steps:
                    b = i + off
                    if kind == "exp":
                        g, kt, p = a
                        e, n = e_of(g, kt, p), e_cols(kt)
                        act.wait_ge(e_ready, b * (NG * TB * PAIRS) + e + 1)
                        need(act, pv_done, b * (NG * TB) + g * TB + kt - 1)
                        nc.scalar.activation(probs[:, e % NP_BUF, :, 0:n], pS[:, :, 0:n], ACT.Exp,
                                             scale=SCALE).then_inc(exp_done, 1)
                    elif kind == "neg_max":
                        g, = a
                        act.wait_ge(nt_ready, b * NG + g + 1)
                        need(act, nm_saved, (b * NG + g) * 32)
                        act.wait_ge(v_ready, (b + 1) * TB)
                        nc.scalar.activation(nm_hi[:], ring[0:G, BANKS[kind, off, a]], ACT.Identity,
                                             scale=-1.0).then_inc(nm_hi_done, 1)
                    elif kind == "qk":
                        g, = a
                        act.wait_ge(qk_ready, b * NG + g + 1)
                        need(act, qk_saved, (b * NG + g) * 32)
                        if g == 0 and i is not None:
                            need(act, ffn_full, (b - 1) * KB)
                        nc.scalar.activation(c_hi[:], ring[:, BANKS[kind, off, a]], ACT.Identity,
                                             bias=bqk_c[:, g:g + 1]).then_inc(qk_hi, 1)
                    elif kind == "v":
                        kt, = a
                        act.wait_ge(v_ready, b * TB + kt + 1)
                        need(act, pv_done, b * (NG * TB))
                        if isinstance(b, int) and b == 0:
                            act.wait_ge(consts, N_CONSTS)
                        nc.scalar.activation(
                            Vo[:, kt, :, 0:D], ring[:, BANKS[kind, off, a], 0:C].rearrange("p (h d) -> p h d", d=D),
                            ACT.Copy).then_inc(v_copied, 1)
                    elif kind == "o_out":
                        g, = a
                        act.wait_ge(pv_done, b * (NG * TB) + (g + 1) * TB)
                        need(act, o_moved, (b * NG + g) * 80)
                        if g == 0:
                            need(act, r_ready, b * CB)
                        nc.scalar.activation(Osb[:], pO[:], ACT.Copy).then_inc(o_out, 1)
                    elif kind == "x1_turn":
                        c, = a
                        act.wait_ge(xt_ready, b * CB + c + 1)
                        need(act, u_ready, b * KB)
                        nc.scalar.activation(x1Thi[:, c], ring[:, BANKS[kind, off, a]], ACT.Copy).then_inc(x1_hi, 1)
                    elif kind == "gate":
                        j, = a
                        act.wait_ge(g_ready, b * KB + j + 1)
                        need(act, ffn_full, b * KB + j)
                        if j == 0:
                            act.wait_ge(qk_saved, (b + 2 if not isinstance(b, int) else min(b + 2, B)) * (NG * 32))
                        nc.scalar.activation(th[:], ring[:, BANKS[kind, off, a]], ACT.Tanh,
                                             scale=s1_c[:, j:j + 1]).then_inc(tanh_done, 1)
                    elif kind == "ffn_hi":
                        j, = a
                        act.wait_ge(ffn_full, b * KB + j + 1)
                        need(act, f_ready, b * 2)
                        nc.scalar.activation(Xhi[:, j], full[:, j % 2], ACT.Copy).then_inc(x_hi, 1)
                    elif kind in ("h1", "h2"):
                        half, j = a
                        u = u_of(kind, half, j)
                        act.wait_ge(h_ready, b * 32 + u + 1)
                        if u < 2:
                            act.wait_ge(x_lo, (b + 1) * KB)
                        else:
                            act.wait_ge(h_lo, b * 32 + u - 1)
                        if u == 0:
                            act.wait_ge(pv_done, (b + 2 if not isinstance(b, int) else min(b + 2, B)) * (NG * TB))
                        src = ring[:, BANKS[kind, off, a], 0:HALF]
                        if kind == "h1":
                            hi, sc = Yhi[:, j], sh1_c[:, j:j + 1]
                        else:
                            hi, sc = Xhi[:, j, half * HALF:(half + 1) * HALF], sh2_c[:, j:j + 1]
                        nc.scalar.activation(hi, src, ACT.Gelu, scale=sc)
                        nc.scalar.activation(full[:, u % 2, 0:HALF], src, ACT.Gelu, scale=sc).then_inc(h_full, 1)

            pipeline(act, work)

        @block.vector
        def _(dve):
            nc.vector.memset(pO[:], 0.0).then_inc(setup_v, 1)
            dve.wait_ge(params_in, 16 * N_PARAMS)
            dve.wait_ge(consts, N_CONSTS)
            nc.vector.tensor_scalar(s1_c, s1_c, 0.5, None, ALU.mult).then_inc(setup_v, 1)
            for c in range(CB):
                spread = nc.vector.tensor_scalar(full[:, c, 0:P], ident[:], 0.0, bv_c[:, c:c + 1], ALU.mult, ALU.add)
            spread.then_inc(setup_v, 1)
            dve.wait_ge(setup_v, 3)
            nc.vector.tensor_tensor(s2_c, s2_c, s1_c, ALU.mult)
            dve.wait_ge(setup_t, 1)
            nc.vector.tensor_tensor(b_tot[:], pM[:, 0, 0:C], b_tot[:], ALU.add).then_inc(setup_v, 1)

            def weight_bits():
                dve.wait_ge(weights_in, 16 * len(FFN))
                n, done = 0, 4
                for w in FFN:
                    words = w[:].bitcast(I32).rearrange("p k n -> p (k n)")
                    for at in range(0, words.shape[1], KB * T):
                        m = min(KB * T, words.shape[1] - at)
                        dve.wait_ge(setup_v, done)
                        nc.vector.tensor_scalar(low[:, 0:m], words[:, at:at + m], LOW_BITS, None,
                                                ALU.bitwise_and).then_inc(setup_v, 1)
                        done += 1
                        dve.wait_ge(setup_v, done)
                        nc.vector.tensor_reduce(lowmax[:, n:n + 1], low[:, 0:m], AX_X, ALU.max).then_inc(setup_v, 1)
                        done += 1
                        n += 1
                dve.wait_ge(setup_v, done)
                nc.vector.tensor_reduce(lowmax[:, 15:16], lowmax[:, 0:n], AX_X, ALU.max).then_inc(setup_v, 1)
                dve.wait_ge(setup_t, 2)
                nc.vector.tensor_copy(flag[:], pM[0:1, 0, 0:1]).then_inc(setup_v, 1)

            def work(i, steps):
                for kind, off, a in steps:
                    b = i + off
                    if kind == "max":
                        g, t, p = a
                        n = m_cols(t)
                        dve.wait_ge(m_ready, b * (NG * TB * PAIRS) + (g * TB + TB - 1 - t) * PAIRS + p + 1)
                        need(dve, nt_ready, b * NG + g)
                        held(dve)
                        for s in range(2):
                            rows = nc.vector.tensor_tensor_reduce(
                                pM[:, s, 0:n], pM[:, s, 0:n], mask[:, T - n:T], 1.0, NEG, ALU.add, ALU.max,
                                mx[:, t, 2 * p + s:2 * p + s + 1])
                        rows.then_inc(m_done, 1)
                    elif kind == "neg_max":
                        g, = a
                        dve.wait_ge(nm_hi_done, b * NG + g + 1)
                        nc.vector.scalar_tensor_tensor(
                            out=nm_lo[:], in0=ring[0:G, BANKS[kind, off, a]], scalar=-1.0, in1=nm_hi[:].bitcast(F32),
                            op0=ALU.mult, op1=ALU.subtract).then_inc(nm_lo_done, 1)
                    elif kind == "qk":
                        g, = a
                        dve.wait_ge(qk_hi, b * NG + g + 1)
                        nc.vector.scalar_tensor_tensor(
                            out=c_lo[:], in0=ring[:, BANKS[kind, off, a]], scalar=bqk_c[:, g:g + 1],
                            in1=c_hi[:].bitcast(F32), op0=ALU.add, op1=ALU.subtract).then_inc(qk_lo, 1)
                    elif kind == "x1_turn":
                        c, = a
                        dve.wait_ge(x1_hi, b * CB + c + 1)
                        nc.vector.tensor_tensor(x1Tlo[:, c], ring[:, BANKS[kind, off, a]], x1Thi[:, c].bitcast(F32),
                                                ALU.subtract).then_inc(x1_lo, 1)
                    elif kind == "up":
                        j, = a
                        dve.wait_ge(tanh_done, b * KB + j + 1)
                        dve.wait_ge(u_ready, b * KB + j + 1)
                        nc.vector.scalar_tensor_tensor(out=th[:], in0=th[:], scalar=1.0, in1=ring[:, BANKS[kind, off, a]],
                                                       op0=ALU.add, op1=ALU.mult).then_inc(gated, 1)
                        dve.wait_ge(gated, b * KB + j + 1)
                        if j >= 2:
                            dve.wait_ge(x_lo, b * KB + j - 1)
                        nc.vector.scalar_tensor_tensor(out=full[:, j % 2], in0=ring[:, BANKS["gate", off, a]],
                                                       scalar=s2_c[:, j:j + 1], in1=th[:],
                                                       op0=ALU.mult, op1=ALU.mult).then_inc(ffn_full, 1)
                    elif kind in ("h1", "h2"):
                        half, j = a
                        u = u_of(kind, half, j)
                        dve.wait_ge(h_full, b * 32 + u + 1)
                        if kind == "h1":
                            hi, lo = Yhi[:, j], Ylo[:, j]
                        else:
                            hi, lo = (X[:, j, half * HALF:(half + 1) * HALF] for X in (Xhi, Xlo))
                        nc.vector.tensor_tensor(lo, full[:, u % 2, 0:HALF], hi.bitcast(F32),
                                                ALU.subtract).then_inc(h_lo, 1)
                    elif kind == "den":
                        dve.wait_ge(den_in, (b + 1) * 16)
                        need(dve, rec_saved, b * 16)
                        nc.vector.reciprocal(rc[:], dn[:]).then_inc(rc_done, 1)
                    elif kind == "den_turn":
                        for m in range(CB):
                            dve.wait_ge(r_ready, b * CB + m + 1)
                            nc.vector.tensor_tensor(Oc[:, m], Oc[:, m], ring[:, BANKS[kind, off, (m,)]],
                                                    ALU.mult).then_inc(o_norm, 1)
                    elif kind == "y":
                        half, = a
                        rows = xr[:, 2 * half:2 * half + 2]
                        dve.wait_ge(y_ready, b * 2 + half + 1)
                        dve.wait_ge(xr_ready, b + 1)
                        nc.vector.tensor_tensor(rows, ring[:, BANKS[kind, off, a]].rearrange("p (t c) -> p t c", c=C),
                                                rows, ALU.add).then_inc(ln1, 1)
                        dve.wait_ge(ln1, b * LN1 + 2 * half + 1)
                        for t in (2 * half, 2 * half + 1):
                            st = nc.vector.bn_stats(st1[:, t], xr[:, t])
                        st.then_inc(ln1, 1)
                    elif kind == "ln1_stats":
                        dve.wait_ge(ln1, b * LN1 + 4)
                        held(dve)
                        for t in range(TB):
                            mv = nc.vector.bn_aggr(mv1[:, t], st1[:, t])
                        mv.then_inc(ln1, 1)
                        dve.wait_ge(ln1, b * LN1 + 5)
                        nc.vector.tensor_scalar(rs1[:], mv1[:, :, 1], EPS, None, ALU.add).then_inc(ln1, 1)
                    elif kind == "ln1":
                        dve.wait_ge(ln1_pow, b + 1)
                        need(dve, xt_ready, b * CB)
                        for t in range(TB):
                            row = nc.vector.tensor_scalar(x1[:, t], xr[:, t], mv1[:, t, 0:1], rs1[:, t:t + 1],
                                                          ALU.subtract, ALU.mult)
                        row.then_inc(ln1, 1)
                    elif kind == "ffn_out":
                        half, = a
                        at = b * LN2 + 6 * half
                        dve.wait_ge(f_ready, b * 2 + half + 1)
                        need(dve, stored, (b * 2 + half) * 16)
                        for t in range(2):
                            scaled = nc.vector.tensor_tensor(z[:, t], ring[:, BANKS[kind, off, a], t * C:(t + 1) * C],
                                                             s3b[:], ALU.mult)
                        scaled.then_inc(ln2, 1)
                        dve.wait_ge(ln2, at + 1)
                        nc.vector.tensor_tensor(z[:], z[:], x1[:, 2 * half:2 * half + 2], ALU.add).then_inc(ln2, 1)
                        dve.wait_ge(ln2, at + 2)
                        for t in range(2):
                            st = nc.vector.bn_stats(st2[:, t], z[:, t])
                        st.then_inc(ln2, 1)
                        dve.wait_ge(ln2, at + 3)
                        held(dve)
                        for t in range(2):
                            mv = nc.vector.bn_aggr(mv2[:, t], st2[:, t])
                        mv.then_inc(ln2, 1)
                        dve.wait_ge(ln2, at + 4)
                        nc.vector.tensor_scalar(rs2[:], mv2[:, :, 1], EPS, None, ALU.add).then_inc(ln2, 1)
                    elif kind == "ln2":
                        half, = a
                        dve.wait_ge(ln2_pow, b * 2 + half + 1)
                        for t in range(2):
                            row = nc.vector.tensor_scalar(z[:, t], z[:, t], mv2[:, t, 0:1], rs2[:, t:t + 1],
                                                          ALU.subtract, ALU.mult)
                        row.then_inc(ln2, 1)

            for i in (-1, 0, 1, 2):
                work(i, steps_of(i))
                if i == 0:
                    weight_bits()
            with dve.Fori(3, B - 1) as i:
                work(i, steps_of(None))
            for i in (B - 1, B):
                work(i, steps_of(i))

        @block.tensor
        def _(pe):
            RELEASE = {
                "qk": lambda g: (qk_lo, NG, g + 1),
                "v": lambda kt: (v_copied, TB, kt + 1),
                "gate": lambda j: (ffn_full, KB, j + 1),
                "up": lambda j: (gated, KB, j + 1),
                "h1": lambda half, j: (h_full, 32, u_of("h1", half, j) + 1),
                "h2": lambda half, j: (h_full, 32, u_of("h2", half, j) + 1),
                "ffn_out": lambda half: (ln2, LN2, 6 * half + 1),
                "y": lambda half: (ln1, LN1, 2 * half + 1),
                "x1_turn": lambda c: (x1_lo, CB, c + 1),
                "neg_max": lambda g: (nm_lo_done, NG, g + 1),
                "den_turn": lambda m: (o_norm, CB, m + 1),
            }

            def iteration(i, steps, taken, general):

                def bank(kind, off, a):
                    n = BANKS[kind, off, a]
                    if n in taken:
                        last, last_off, last_a = taken[n]
                        s, per, nth = RELEASE[last](*last_a)
                        pe.wait_ge(s, (i + last_off) * per + nth)
                    taken[n] = (kind, off, a)
                    return ring[:, n]

                def parts(w, act):
                    return (w.bitcast(F32), act.bitcast(F32)) if general else (w, act)

                for kind, off, a in steps:
                    b = i + off
                    if kind == "exp":
                        g, kt, p = a
                        n, slot = e_cols(kt), g % 2
                        if kt == 0 and p == 0:
                            pe.wait_ge(nm_in, (b * NG + g + 1) * 32)
                        need(pe, exp_done, b * (NG * TB * PAIRS) + e_of(g, kt, p))
                        for s in range(2):
                            rows = slice(64 * s, 64 * s + EROWS)
                            mm = nc.tensor.matmul(pS[:, s, 0:n], Ks[rows, slot, p, kt * P:(kt + 1) * P],
                                                  Qs[rows, slot, p, kt * P:T], start=True, stop=True)
                        mm.then_inc(e_ready, 1)
                    elif kind == "max":
                        g, t, p = a
                        n, slot = m_cols(t), g % 2
                        nth = b * (NG * TB * PAIRS) + (g * TB + TB - 1 - t) * PAIRS + p
                        if t == TB - 1 and p == 0:
                            pe.wait_ge(stack_in[slot], (b * 2 + g // 2 + 1) * 192)
                        need(pe, m_done, nth)
                        for s in range(2):
                            rows = slice(64 * s, 64 * s + SROWS)
                            mm = nc.tensor.matmul(pM[:, s, 0:n], Qs[rows, slot, p, t * P:(t + 1) * P],
                                                  Ks[rows, slot, p, 0:n], start=True, stop=True)
                        mm.then_inc(m_ready, 1)
                    elif kind == "neg_max":
                        g, = a
                        pe.wait_ge(m_done, b * (NG * TB * PAIRS) + (g + 1) * TB * PAIRS)
                        to = bank(kind, off, a)
                        for t in range(TB):
                            mm = nc.tensor.transpose(to[0:G, t * P:(t + 1) * P], mx[:, t], ident[:])
                        mm.then_inc(nt_ready, 1)
                    elif kind == "pv":
                        g, kt = a
                        n = e_cols(kt)
                        if kt == 0:
                            if g == 0:
                                pe.wait_ge(v_copied, (b + 1) * TB)
                            need(pe, o_out, b * NG + g)
                        pe.wait_ge(mask_done, b * (NG * TB * PAIRS) + e_of(g, kt, PAIRS - 1) + 1)
                        for p in range(PAIRS):
                            for s in range(2):
                                j = 2 * p + s
                                mm = nc.tensor.matmul(pO[32 * j:32 * j + VW, kt * P:T], Vo[:, kt, G * g + j],
                                                      probs[:, e_of(g, kt, p) % NP_BUF, s, 0:n],
                                                      start=(kt == 0), stop=(kt == TB - 1))
                        mm.then_inc(pv_done, 1)
                    elif kind == "qk":
                        g, = a
                        pe.wait_ge(xT_in, (b + 1) * 16)
                        to = bank(kind, off, a)
                        for c in range(CB):
                            mm = nc.tensor.matmul(to, Wqk[:, c, g], xTs[:, c], start=(c == 0), stop=(c == CB - 1))
                        mm.then_inc(qk_ready, 1)
                    elif kind == "v":
                        kt, = a
                        to = bank(kind, off, a)
                        for c in range(CB):
                            mm = nc.tensor.matmul(to[:, 0:C], xTs[:, c, kt * P:(kt + 1) * P], Wv[:, c],
                                                  start=(c == 0), stop=(c == CB - 1))
                        mm.then_inc(v_ready, 1)
                    elif kind == "den_turn":
                        pe.wait_ge(rec_in, (b + 1) * 16)
                        for m in range(CB):
                            to = bank(kind, off, (m,))
                            nc.tensor.matmul(to, sel[:, m], Osb[0:H], start=True, stop=True).then_inc(r_ready, 1)
                    elif kind == "y":
                        half, = a
                        pe.wait_ge(o_norm, (b + 1) * CB)
                        to = bank(kind, off, a)
                        for t in range(2):
                            tok = slice((2 * half + t) * P, (2 * half + t + 1) * P)
                            for c in range(CB):
                                mm = nc.tensor.matmul(to[:, t * C:(t + 1) * C], Oc[:, c, tok], Wout[:, c],
                                                      start=(c == 0), stop=(c == CB - 1))
                        mm.then_inc(y_ready, 1)
                    elif kind == "x1_turn":
                        c, = a
                        pe.wait_ge(ln1, (b + 1) * LN1)
                        to = bank(kind, off, a)
                        for t in range(TB):
                            mm = nc.tensor.transpose(to[:, t * P:(t + 1) * P], x1[:, t, c * P:(c + 1) * P], ident[:])
                        mm.then_inc(xt_ready, 1)
                    elif kind in ("gate", "up"):
                        j, = a
                        W, done = (W1, g_ready) if kind == "gate" else (W2, u_ready)
                        pe.wait_ge(x1_lo, (b + 1) * CB)
                        to = bank(kind, off, a)
                        for c in range(CB):
                            for X in (x1Thi, x1Tlo):
                                w, x_part = parts(W[:, c, j * P:(j + 1) * P], X[:, c])
                                mm = nc.tensor.matmul(to, w, x_part, start=(c == 0 and X is x1Thi),
                                                      stop=(c == CB - 1 and X is x1Tlo))
                        mm.then_inc(done, 1)
                    elif kind in ("h1", "h2"):
                        half, j = a
                        W, src = (H1, (Xhi, Xlo)) if kind == "h1" else (H2, (Yhi, Ylo))
                        tok = slice(half * HALF, (half + 1) * HALF) if kind == "h1" else slice(0, HALF)
                        if kind == "h1":
                            pe.wait_ge(x_lo, (b + 1) * KB)
                        else:
                            pe.wait_ge(h_lo, b * 32 + half * 16 + KB)
                        to = bank(kind, off, a)[:, 0:HALF]
                        for k in range(KB):
                            for m, X in enumerate(src):
                                w, x_part = parts(W[:, k, j * P:(j + 1) * P], X[:, k, tok])
                                mm = nc.tensor.matmul(to, w, x_part, start=(k == 0 and m == 0),
                                                      stop=(k == KB - 1 and m == 1))
                        mm.then_inc(h_ready, 1)
                    elif kind == "ffn_out":
                        half, = a
                        pe.wait_ge(h_lo, b * 32 + half * 16 + 2 * KB)
                        to = bank(kind, off, a)
                        for t in range(2):
                            tok = slice((2 * half + t) * P, (2 * half + t + 1) * P)
                            for k in range(KB):
                                for m, X in enumerate((Xhi, Xlo)):
                                    w, x_part = parts(W3[:, k], X[:, k, tok])
                                    mm = nc.tensor.matmul(to[:, t * C:(t + 1) * C], x_part, w,
                                                          start=(k == 0 and m == 0), stop=(k == KB - 1 and m == 1))
                        mm.then_inc(f_ready, 1)
                for n, (kind, off, a) in taken.items():
                    taken[n] = (kind, off - 1, a)

            def ffn_iterations(taken, general):
                for i in (1, 2):
                    iteration(i, steps_of(i), taken, general)
                with pe.Fori(3, B - 1) as i:
                    iteration(i, steps_of(None), taken, general)
                for i in (B - 1, B):
                    iteration(i, steps_of(i), taken, general)

            pe.wait_ge(params_in, 16 * N_PARAMS)
            pe.wait_ge(setup_v, 3)
            for c in range(CB):
                mm = nc.tensor.matmul(pM[:, 0, 0:C], full[:, c, 0:P], Wout[:, c], start=(c == 0), stop=(c == CB - 1))
            mm.then_inc(setup_t, 1)
            pe.wait_ge(setup_v, 4)
            taken = {}
            for i in (-1, 0):
                iteration(i, steps_of(i), taken, False)
            chunks = sum(-(-w.shape[1] * w.shape[2] // (KB * T)) for w in FFN)
            pe.wait_ge(setup_v, 4 + 2 * chunks + 1)
            nc.tensor.matmul(pM[0:1, 0, 0:1], lowmax[:, 15:16], ones_c[:], start=True, stop=True).then_inc(setup_t, 1)
            pe.wait_ge(setup_v, 4 + 2 * chunks + 2)
            has_low_bits = pe.value_load(flag[0:1, 0:1], min_val=0, max_val=1 << 20)
            with pe.If(has_low_bits > 0):
                ffn_iterations(dict(taken), True)
            with pe.Else():
                ffn_iterations(dict(taken), False)


def kernel(**inputs):
    import concourse.bacc as bacc
    from concourse.bass_utils import run_bass_kernel_spmd

    a = {k: np.asarray(v) for k, v in inputs.items()}
    x = a["L0_attn_x"]
    w_qkv, b_qkv = a["L0_attn_Wqkv"], a["L0_attn_bqkv"]
    w_qk = np.ascontiguousarray(w_qkv[:, :2 * C].reshape(C, 2, NG, G * D).transpose(0, 2, 1, 3)).reshape(C, NG, P)
    b_qk = b_qkv[:2 * C].reshape(2, NG, G * D).transpose(1, 0, 2).reshape(NG, P)
    cols = np.zeros((P, 40), np.float32)
    cols[:, 0:4] = b_qk.T
    cols[:, 4:6] = b_qkv[2 * C:].reshape(CB, P).T
    for n, name in enumerate(("w1_s", "w2_s", "h1_s", "h2_s")):
        cols[:, 8 * n + 8:8 * n + 16] = a["L0_ffn_" + name].reshape(KB, P).T
    arrays = {
        "x": np.ascontiguousarray(x),
        "xT": np.ascontiguousarray(x.transpose(0, 2, 1)),
        "w_qk": w_qk,
        "w_v": np.ascontiguousarray(w_qkv[:, 2 * C:]),
        "w_out": np.ascontiguousarray(a["L0_attn_Wout"]),
    }
    for name in ("w1", "w2", "h1", "h2", "w3"):
        arrays[name] = np.ascontiguousarray(a[f"L0_ffn_{name}_w"].T)
    arrays["cols"] = cols
    arrays["b_out"] = np.ascontiguousarray(a["L0_attn_bout"])
    arrays["s3"] = np.ascontiguousarray(a["L0_ffn_w3_s"])

    nc = bacc.Bacc("TRN2", target_bir_lowering=False, num_devices=1)
    args = {n: nc.dram_tensor(f"in_{n}", v.shape, F32, kind="ExternalInput").ap() for n, v in arrays.items()}
    out = nc.dram_tensor("out_0", (B, T, C), F32, kind="ExternalOutput").ap()
    build(nc, args["x"], args["xT"], args["w_qk"], args["w_v"], args["w_out"],
          [args[n] for n in ("w1", "w2", "h1", "h2", "w3")], args["cols"], args["b_out"], args["s3"], out)
    got = run_bass_kernel_spmd(nc, [{f"in_{n}": v for n, v in arrays.items()}], core_ids=[0])
    return got.results[0]["out_0"]
```

```python
from contextlib import ExitStack

import numpy as np

import concourse.bass as bass
from concourse import mybir

F32 = mybir.dt.float32
F32R = mybir.dt.float32r
BF16 = mybir.dt.bfloat16
I32 = mybir.dt.int32
ACT = mybir.ActivationFunctionType
ALU = mybir.AluOpType
AX_X = mybir.AxisListType.X

P = 128
B, T, C = 16, 512, 256
H = 16
D = C // H
HID = 1024
SCALE = float(D) ** -0.5
EPS = 1e-5
NEG = -3.0e38
LOW_CHUNK = 2048
LOW_BITS = 0xFFF

CB = C // P
KB = HID // P
TB = T // P
HALF = T // 2
G = 4
NG = H // G
PAIRS = G // 2
PARTS = 4
SROWS = PARTS * D
NM_ROWS = 32 + G
VW = D + 1
NP_BUF = 4
MISC = 3


def plan_iteration():
    steps = []

    def add(kind, off, *args):
        steps.append((kind, off, args))

    def exps(g, between):
        e = 0
        for kt in range(TB):
            for p in range(PAIRS):
                add("exp", 0, g, kt, p)
                steps.extend(between.get(e, []))
                e += 1
            if kt:
                add("pv", 0, g, kt - 1)

    def last_pv(g):
        add("pv", 0, g, TB - 1)
        add("o_out", 0, g)
        add("stack", 0 if g + 2 < NG else 1, (g + 2) % NG)

    def hidden(layer, off, half, after):
        for j in range(KB):
            add(layer, off, half, j)
            if "pv" in after.get(j, []):
                last_pv(after[j][1])
                steps.extend(after[j][2:])
            else:
                steps.extend(after.get(j, []))
            add("h_rest", off, layer, half, j)

    def maxes(off, g):
        return [("max", off, (g, t, p)) for t in reversed(range(TB)) for p in range(PAIRS)]

    def gated(off, half, at, others):
        between = {e: list(more) for e, more in others.items()}
        for e, n in at:
            between.setdefault(e, []).append(("gu", off, (half, n)))
            if n:
                between[e].append(("ffn_hi", off, (half, n - 1)))
        return between

    m = maxes(0, 1)
    add("y", -1, 0)
    exps(0, {0: [("y", -1, (1,))], 2: [("ln1_stats", -1, ())], 3: [("qk", 0, (3,))], 4: [m[0]], 5: [m[1]], 6: [m[2]]})
    hidden("h2", -2, 1, {0: ["pv", 0, m[3]], 1: [m[4]], 2: [m[5]], 3: [m[6], m[7]], 4: [("neg_max", 0, (1,))]})
    add("ffn_out", -2, 1)
    add("ln1", -1)
    add("ln2_stats", -2, 1)
    add("load_xT", 1)
    m = maxes(0, 2)
    steps.append(m[0])
    exps(1, gated(-1, 0, [(3, 0), (4, 1), (4, 2), (5, 3), (5, 4), (6, 5), (7, 6), (7, 7)],
                  {0: [m[1]], 1: [("x1_turn", -1, (0,))], 2: [("x1_turn", -1, (1,)), ("ln2", -2, (1,))]}))
    add("load_x", 0)
    steps.append(m[2])
    add("ffn_hi", -1, 0, KB - 1)
    last_pv(1)
    hidden("h1", -1, 0, {0: [m[3]], 1: [m[4]], 2: [m[5]], 3: [m[6], m[7]], 4: [("neg_max", 0, (2,))]})
    m = maxes(0, 3)
    add("qk", 1, 0)
    exps(2, {e + 2: [m[e]] for e in range(4)})
    hidden("h2", -1, 0, {0: ["pv", 2, m[4]], 1: [m[5]], 2: [m[6], m[7]], 3: [("neg_max", 0, (3,)), ("qk", 1, (1,))]})
    add("ffn_out", -1, 0)
    add("ln2_stats", -1, 0)
    m = maxes(1, 0)
    add("gu", -1, 1, 0)
    exps(3, gated(-1, 1, [(1, 1), (2, 2), (3, 3), (4, 4), (5, 5), (6, 6), (7, 7)], {3: [("ln2", -1, (0,))]}))
    steps.append(m[0])
    add("ffn_hi", -1, 1, KB - 1)
    last_pv(3)
    add("qk", 1, 2)
    hidden("h1", -1, 1, {0: [m[1], ("v", 1, (0,)), ("den", 0, ())], 1: [m[2], ("v", 1, (1,))],
                         2: [m[3], ("v", 1, (2,)), ("rec_save", 0, ())], 3: [m[4], ("v", 1, (3,)), ("rec_load", 0, ())],
                         4: [m[5], m[6], m[7]], 5: [("neg_max", 1, (0,))], 7: [("den_turn", 0, ())]})
    return steps


STEPS = plan_iteration()
BANKED = [s for s in STEPS if s[0] in
          ("qk", "v", "gu", "h1", "h2", "ffn_out", "y", "x1_turn", "neg_max")]


def ring_banks():
    at, banks = 0, {}
    for kind, off, args in STEPS:
        n = 2 if kind == "den_turn" else 1 if (kind, off, args) in BANKED else 0
        for m in range(n):
            key = (kind, off, args + (m,)) if kind == "den_turn" else (kind, off, args)
            banks[key] = at % MISC
            at += 1
    return banks


BANKS = ring_banks()


def steps_of(i):
    return [s for s in STEPS if i is None or 0 <= i + s[1] < B]


def over(nc, base, name, shape, dt):
    return nc.alloc_sbuf_tensor_at(name, shape, dt, offset=base)


def build(nc, x, xT, w_qk, w_v, w_out, w_ffn, cols_in, b_out, s3, out):
    with ExitStack() as ctx:
        def sb(name, shape, dt=F32):
            return ctx.enter_context(nc.sbuf_tensor(name, shape, dt))

        def psum(name, shape):
            return ctx.enter_context(nc.psum_tensor(name, shape, F32))

        def sem(name):
            return ctx.enter_context(nc.semaphore(name))

        def dram(name, shape):
            return nc.dram_tensor(name, shape, F32, kind="Internal").ap()

        W1 = sb("W1", [P, CB, HID], F32R)
        W2 = sb("W2", [P, CB, HID], F32R)
        H1 = sb("H1", [P, KB, HID], F32R)
        H2 = sb("H2", [P, KB, HID], F32R)
        W3 = sb("W3", [P, KB, C], F32R)
        FFN = (W1, W2, H1, H2, W3)
        Wqk = sb("Wqk", [P, CB, NG, P])
        Wv = sb("Wv", [P, CB, C])
        Wout = sb("Wout", [P, CB, C])
        Qs = sb("Qs", [P, 2, PAIRS, T], F32R)
        Ks = sb("Ks", [P, 2, PAIRS, T], F32R)
        Vo = sb("Vo", [P, TB, H, VW])
        Osb = sb("Osb", [P, T])
        Oc = sb("Oc", [P, CB, T])
        low_at = nc.sbuf_base
        Xhi = sb("Xhi", [P, KB, HALF], F32R)
        low = over(nc, low_at, "low_bits", [P, LOW_CHUNK], I32)
        Xlo = sb("Xlo", [P, KB, HALF], F32R)
        Yhi = sb("Yhi", [P, KB, HALF], F32R)
        Ylo = sb("Ylo", [P, KB, HALF], F32R)
        x1Thi = sb("x1Thi", [P, CB, T], F32R)
        x1Tlo = sb("x1Tlo", [P, CB, T], F32R)
        full_g = sb("full_g", [P, 2, HALF])
        full_h = sb("full_h", [P, 2, HALF])
        xr = sb("xr", [P, TB, C])
        x1 = sb("x1", [P, TB, C])
        z = sb("z", [P, 2, C])
        probs = sb("probs", [P, NP_BUF, 2, T])
        c_at = nc.sbuf_base
        c_hi = sb("c_hi", [P, T], F32R)
        th = over(nc, c_at, "th", [P, 2, HALF], F32)
        c_lo = sb("c_lo", [P, T], F32R)
        xTs = sb("xTs", [P, CB, T])
        nm = sb("nm", [NM_ROWS, T], F32R)
        mask = sb("mask", [P, T], BF16)
        ident = sb("ident", [P, P])
        sel = sb("sel", [H, CB, P])
        b_tot = sb("b_tot", [P, C])
        s3b = sb("s3b", [P, C])
        cols = sb("cols", [P, 40])
        bqk_c, bv_c = cols[:, 0:NG], cols[:, 4:6]
        s1_c, s2_c, sh1_c, sh2_c = (cols[:, 8 * n:8 * n + 8] for n in (1, 2, 3, 4))
        mx = sb("mx", [P, TB, G])
        dn = sb("dn", [P, H * T // P])
        st1, mv1, rs1 = sb("st1", [P, TB, 6]), sb("mv1", [P, TB, 2]), sb("rs1", [P, TB])
        st2, mv2, rs2 = sb("st2", [P, 2, 6]), sb("mv2", [P, 2, 2]), sb("rs2", [P, 2])
        minus_half = sb("minus_half", [P, TB])
        lowmax = sb("lowmax", [P, 1])
        ones_c = sb("ones_c", [P, 1])
        flag = sb("flag", [1, 1], I32)

        pS = psum("pS", [P, 2, T])
        pM = psum("pM", [P, 2, T])
        pO = psum("pO", [P, T])
        ring = psum("ring", [P, MISC, T])

        raw = [dram(f"raw{n}", w.shape) for n, w in enumerate(w_ffn)]
        qk_d = dram("qk_d", [NG, P, PARTS, T])
        den_d = dram("den_d", [H, T])
        rec_d = dram("rec_d", [H, T])

        xT_in, x_in, params_in, raw_in, weights_in = map(sem, ("xT_in", "x_in", "params_in", "raw_in", "weights_in"))
        const_rows, osb_set = sem("const_rows"), sem("osb_set")
        qk_saved, nm_in, o_moved = map(sem, ("qk_saved", "nm_in", "o_moved"))
        stack_in = [sem("stack_in0"), sem("stack_in1")]
        den_in, rec_saved, rec_in, stored = map(sem, ("den_in", "rec_saved", "rec_in", "stored"))
        qk_ready, v_ready, e_ready, m_ready, pv_done = map(sem, ("qk_ready", "v_ready", "e_ready", "m_ready", "pv_done"))
        nt_ready, xt_ready, gu_ready, h_ready = map(sem, ("nt_ready", "xt_ready", "gu_ready", "h_ready"))
        f_ready, y_ready, r_ready = map(sem, ("f_ready", "y_ready", "r_ready"))
        qk_hi, exp_done, tanh_done, x_hi, h_full = map(sem, ("qk_hi", "exp_done", "tanh_done", "x_hi", "h_full"))
        o_out, nm_hi_done, x1_hi, v_copied = map(sem, ("o_out", "nm_hi_done", "x1_hi", "v_copied"))
        qk_lo, m_done, nm_lo_done, gated, ffn_full, h_lo = map(sem, ("qk_lo", "m_done", "nm_lo_done", "gated", "ffn_full", "h_lo"))
        x1_lo, rc_done, o_norm, ln1, ln2 = map(sem, ("x1_lo", "rc_done", "o_norm", "ln1", "ln2"))
        mask_done, x_lo, xr_ready, ln1_pow, ln2_pow = map(sem, ("mask_done", "x_lo", "xr_ready", "ln1_pow", "ln2_pow"))
        consts, setup_v, setup_t, passed = map(sem, ("consts", "setup_v", "setup_t", "passed"))

        LN1, LN2 = 7, 12
        N_PARAMS = 6
        SAVES = 16 * 5
        N_CONSTS = 9

        def need(eng, s, n):
            if not (isinstance(n, int) and n <= 0):
                eng.wait_ge(s, n)

        def held(eng):
            eng.sem_inc(passed, 1)

        def pipeline(eng, body):
            for i in (-1, 0, 1, 2):
                body(i, steps_of(i))
            with eng.Fori(3, B - 1) as i:
                body(i, steps_of(None))
            for i in (B - 1, B, B + 1):
                body(i, steps_of(i))

        def e_of(g, kt, p):
            return (g * TB + kt) * PAIRS + p

        HEADS = NG * TB * G

        def u_of(kind, half, j):
            return (2 * half + (kind == "h2")) * KB + j

        def e_cols(kt):
            return T - kt * P

        def m_cols(t):
            return (t + 1) * P

        block = ctx.enter_context(nc.Block())

        @block.sync
        def _(sp):
            sp.dma_start(Wqk[:], w_qk.rearrange("(c p) g n -> p c g n", p=P)).then_inc(params_in, 16)
            sp.dma_start(cols[:], cols_in).then_inc(params_in, 16)
            sp.dma_start(xTs[:], xT[0].rearrange("(c p) t -> p c t", p=P)).then_inc(xT_in, 16)
            sp.wait_ge(osb_set, 2)
            for g in range(NG):
                sp.dma_start(qk_d[g, :, PARTS - 1], Osb[:]).then_inc(const_rows, 16)
            sp.dma_start(Wv[:], w_v.rearrange("(c p) n -> p c n", p=P)).then_inc(params_in, 16)
            sp.dma_start(Wout[:], w_out.rearrange("(c p) n -> p c n", p=P)).then_inc(params_in, 16)
            sp.dma_start(b_tot[:], b_out.rearrange("(a n) -> a n", a=1).broadcast_to([P, C])).then_inc(params_in, 16)
            sp.dma_start(s3b[:], s3.rearrange("(a n) -> a n", a=1).broadcast_to([P, C])).then_inc(params_in, 16)

            def move(i, steps):
                for kind, off, a in steps:
                    b = i + off
                    if kind == "load_xT" and not (isinstance(b, int) and b == 0):
                        sp.wait_ge(qk_ready, b * NG)
                        held(sp)
                        sp.dma_start(xTs[:], xT[bass.ds(b, 1)].rearrange("a (c p) t -> p (a c) t", p=P)).then_inc(xT_in, 16)
                    elif kind == "load_x":
                        if isinstance(b, int) and b == 0:
                            sp.wait_ge(raw_in, 16 * len(FFN))
                            for w, r in zip(FFN, raw):
                                sp.dma_start(w[:].bitcast(F32), r.rearrange("(k p) n -> p k n", p=P)).then_inc(weights_in, 16)
                        need(sp, ln1, b * LN1)
                        held(sp)
                        sp.dma_start(xr[:], x[bass.ds(b, 1)].rearrange("a (t p) c -> p (a t) c", p=P)).then_inc(x_in, 16)
                    elif kind == "qk":
                        g, = a
                        sp.wait_ge(qk_lo, b * NG + g + 1)
                        for part, src, rows in ((0, c_hi, slice(0, P)), (1, c_hi, slice(0, G * D)), (1, c_lo, slice(G * D, P)),
                                                (2, c_lo, slice(0, G * D)), (2, c_hi, slice(G * D, P))):
                            sp.dma_start(qk_d[g, rows, part], src[rows].bitcast(F32)).then_inc(qk_saved, 16)
                    elif kind == "stack":
                        g, = a
                        slot = g % 2
                        sp.wait_ge(qk_saved, (b * NG + g + 1) * SAVES)
                        held(sp)
                        need(sp, e_ready, b * HEADS + (g - 1) * TB * G)
                        if g < 2 and isinstance(b, int) and b == 0:
                            sp.wait_ge(const_rows, 16 * NG)
                        held(sp)
                        for dst, qk in ((Qs, 0), (Ks, 1)):
                            rows = qk_d[g, qk * G * D:(qk + 1) * G * D].rearrange("(p s d) r n -> (s d r) p n", p=PAIRS, s=2)
                            sp.dma_start(dst[:, slot].bitcast(F32), rows).then_inc(stack_in[slot], 16)
                    elif kind == "neg_max":
                        g, = a
                        sp.wait_ge(nm_lo_done, b * NG + g + 1)
                        for j in range(G):
                            at = 64 * (j % 2) + PARTS - 1
                            sp.dma_start(Qs[at:at + PARTS + 1:PARTS, g % 2, j // 2].bitcast(F32),
                                         nm[j:NM_ROWS:32].bitcast(F32)).then_inc(nm_in, 16)
                    elif kind == "o_out":
                        g, = a
                        sp.wait_ge(o_out, b * NG + g + 1)
                        held(sp)
                        if g == 0:
                            need(sp, y_ready, b * 2)
                        held(sp)
                        for j in range(G):
                            at = 64 * (g % 2) + D * j
                            sp.dma_start(Oc[at:at + D, g // 2], Osb[32 * j:32 * j + D]).then_inc(o_moved, 16)
                        sp.dma_start(den_d[g * G:(g + 1) * G], Osb[D:P:32, :]).then_inc(o_moved, 16)
                    elif kind == "den":
                        sp.wait_ge(o_moved, (b + 1) * (NG * 80))
                        sp.dma_start(dn[:], den_d.rearrange("h (c n) -> (h c) n", n=H * T // P)).then_inc(den_in, 16)
                    elif kind == "rec_save":
                        sp.wait_ge(rc_done, b + 1)
                        sp.dma_start(rec_d.rearrange("h (c n) -> (h c) n", n=H * T // P), dn[:]).then_inc(rec_saved, 16)
                    elif kind == "rec_load":
                        sp.wait_ge(rec_saved, (b + 1) * 16)
                        sp.dma_start(Osb[0:H], rec_d).then_inc(rec_in, 16)
                    elif kind == "ln2":
                        half, = a
                        sp.wait_ge(ln2, b * LN2 + 6 * half + 6)
                        held(sp)
                        sp.dma_start(out[bass.ds(b, 1)].rearrange("a (t p) c -> p (a t) c", p=P)[:, 2 * half:2 * half + 2],
                                     z[:]).then_inc(stored, 16)

            for i in (-1, 0, 1, 2):
                move(i, steps_of(i))
            with sp.Fori(3, B - 1) as i:
                move(i, steps_of(None))
            for i in (B - 1, B, B + 1):
                move(i, steps_of(i))
            sp.wait_ge(stored, B * 32)

        @block.gpsimd
        def _(pool):
            nc.gpsimd.memset(ident[:], 0.0).then_inc(consts, 1)
            nc.gpsimd.memset(mask[:], 0.0).then_inc(consts, 1)
            nc.gpsimd.memset(sel[:], 1.0).then_inc(consts, 1)
            nc.gpsimd.memset(minus_half[:], -0.5).then_inc(consts, 1)
            nc.gpsimd.memset(ones_c[:], 1.0).then_inc(consts, 1)
            nc.gpsimd.memset(Vo[:], 1.0).then_inc(consts, 1)
            pool.wait_ge(consts, 6)
            nc.gpsimd.affine_select(out=ident[:], in_=ident[:], compare_op=ALU.not_equal, fill=1.0, base=0,
                                    pattern=[[-1, P]], channel_multiplier=1).then_inc(consts, 1)
            tri = mask[:, T - P:T]
            nc.gpsimd.affine_select(out=tri, in_=tri, compare_op=ALU.is_ge, fill=NEG, base=0,
                                    pattern=[[-1, P]], channel_multiplier=1).then_inc(consts, 1)
            heads = sel[:].rearrange("h c (e d) -> h (c e) d", d=D)
            nc.gpsimd.affine_select(out=heads, in_=heads, compare_op=ALU.is_equal, fill=0.0, base=0,
                                    pattern=[[-1, H], [0, D]], channel_multiplier=1).then_inc(consts, 1)

            def work(i, steps):
                for kind, off, a in steps:
                    b = i + off
                    if kind == "exp":
                        g, kt, p = a
                        e = e_of(g, kt, p)
                        pool.wait_ge(exp_done, b * HEADS + 2 * e + 2)
                        held(pool)
                        tri_p = probs[:, e % NP_BUF, :, 0:P]
                        nc.gpsimd.affine_select(out=tri_p, in_=tri_p, compare_op=ALU.is_ge, fill=0.0, base=0,
                                                pattern=[[0, 2], [1, P]], channel_multiplier=-1).then_inc(mask_done, 1)
                    elif kind == "ffn_hi":
                        half, j = a
                        pool.wait_ge(x_hi, b * (2 * KB) + half * KB + j + 1)
                        nc.gpsimd.tensor_tensor(Xlo[:, j], full_g[:, j % 2], Xhi[:, j].bitcast(F32),
                                                ALU.subtract).then_inc(x_lo, 1)
                    elif kind == "load_x":
                        if isinstance(b, int) and b == 0:
                            pool.wait_ge(setup_v, 4)
                        pool.wait_ge(x_in, (b + 1) * 16)
                        for t in range(TB):
                            add_b = nc.gpsimd.tensor_tensor(xr[:, t], xr[:, t], b_tot[:], ALU.add)
                        add_b.then_inc(xr_ready, 1)
                    elif kind == "ln1_stats":
                        pool.wait_ge(ln1, b * LN1 + 6)
                        nc.gpsimd.tensor_tensor(rs1[:], rs1[:], minus_half[:], ALU.pow).then_inc(ln1_pow, 1)
                    elif kind == "ln2":
                        half, = a
                        pool.wait_ge(ln2, b * LN2 + 6 * half + 5)
                        nc.gpsimd.tensor_tensor(rs2[:], rs2[:], minus_half[:, 0:2], ALU.pow).then_inc(ln2_pow, 1)

            pipeline(pool, work)

        @block.scalar
        def _(act):
            act.wait_ge(params_in, 16 * N_PARAMS)
            for w, r in zip(w_ffn, raw):
                act.dma_start(r, w).then_inc(raw_in, 16)

            def work(i, steps):
                for kind, off, a in steps:
                    b = i + off
                    if kind == "exp":
                        g, kt, p = a
                        e, n = e_of(g, kt, p), e_cols(kt)
                        need(act, pv_done, b * (NG * TB) + g * TB + kt - 1)
                        for s in range(2):
                            act.wait_ge(e_ready, b * HEADS + 2 * e + s + 1)
                            nc.scalar.activation(probs[:, e % NP_BUF, s, 0:n], pS[:, s, 0:n], ACT.Exp,
                                                 scale=SCALE).then_inc(exp_done, 1)
                    elif kind == "neg_max":
                        g, = a
                        act.wait_ge(nt_ready, b * NG + g + 1)
                        need(act, nm_in, (b * NG + g) * 64)
                        nc.scalar.activation(nm[:], ring[0:NM_ROWS, BANKS[kind, off, a]], ACT.Identity,
                                             scale=-1.0).then_inc(nm_hi_done, 1)
                    elif kind == "qk":
                        g, = a
                        act.wait_ge(qk_ready, b * NG + g + 1)
                        need(act, qk_saved, (b * NG + g) * SAVES)
                        need(act, ffn_full, (b - 2) * (2 * KB) + KB if g < 2 else (b - 1) * (2 * KB))
                        nc.scalar.activation(c_hi[:], ring[:, BANKS[kind, off, a]], ACT.Identity,
                                             bias=bqk_c[:, g:g + 1]).then_inc(qk_hi, 1)
                    elif kind == "v":
                        kt, = a
                        act.wait_ge(v_ready, b * TB + kt + 1)
                        need(act, pv_done, b * (NG * TB))
                        if isinstance(b, int) and b == 0:
                            act.wait_ge(consts, N_CONSTS)
                        nc.scalar.activation(
                            Vo[:, kt, :, 0:D], ring[:, BANKS[kind, off, a], 0:C].rearrange("p (h d) -> p h d", d=D),
                            ACT.Copy).then_inc(v_copied, 1)
                    elif kind == "o_out":
                        g, = a
                        act.wait_ge(pv_done, b * (NG * TB) + (g + 1) * TB)
                        need(act, o_moved, (b * NG + g) * 80)
                        if g == 0:
                            need(act, r_ready, b * CB)
                        nc.scalar.activation(Osb[:], pO[:], ACT.Copy).then_inc(o_out, 1)
                    elif kind == "x1_turn":
                        c, = a
                        act.wait_ge(xt_ready, b * CB + c + 1)
                        need(act, gu_ready, b * (2 * KB))
                        nc.scalar.activation(x1Thi[:, c], ring[:, BANKS[kind, off, a]], ACT.Copy).then_inc(x1_hi, 1)
                    elif kind == "gu":
                        half, j = a
                        n = half * KB + j
                        act.wait_ge(gu_ready, b * (2 * KB) + n + 1)
                        need(act, ffn_full, b * (2 * KB) + n - 1)
                        if j == 0:
                            groups = (b + 2) * NG + 2 * half
                            act.wait_ge(qk_saved, (min(groups, B * NG) if isinstance(b, int) else groups) * SAVES)
                        nc.scalar.activation(th[:, j % 2], ring[:, BANKS[kind, off, a], 0:HALF], ACT.Tanh,
                                             scale=s1_c[:, j:j + 1]).then_inc(tanh_done, 1)
                    elif kind == "ffn_hi":
                        half, j = a
                        act.wait_ge(ffn_full, b * (2 * KB) + half * KB + j + 1)
                        need(act, f_ready, b * 2 + half)
                        nc.scalar.activation(Xhi[:, j], full_g[:, j % 2], ACT.Copy).then_inc(x_hi, 1)
                    elif kind in ("h1", "h2"):
                        half, j = a
                        u = u_of(kind, half, j)
                        act.wait_ge(h_ready, b * 32 + u + 1)
                        need(act, h_lo, b * 32 + u - 1)
                        src = ring[:, BANKS[kind, off, a], 0:HALF]
                        if kind == "h1":
                            hi, sc = Yhi[:, j], sh1_c[:, j:j + 1]
                        else:
                            hi, sc = Xhi[:, j], sh2_c[:, j:j + 1]
                        nc.scalar.activation(hi, src, ACT.Gelu, scale=sc)
                        nc.scalar.activation(full_h[:, u % 2], src, ACT.Gelu, scale=sc).then_inc(h_full, 1)

            pipeline(act, work)

        @block.vector
        def _(dve):
            nc.vector.memset(Osb[0:G * D], 0.0).then_inc(osb_set, 1)
            nc.vector.memset(Osb[G * D:P], 1.0).then_inc(osb_set, 1)
            nc.vector.memset(pO[:], 0.0)
            nc.vector.memset(ring[:], 0.0).then_inc(setup_v, 1)
            dve.wait_ge(params_in, 16 * N_PARAMS)
            dve.wait_ge(consts, N_CONSTS)
            nc.vector.tensor_scalar(s1_c, s1_c, 0.5, None, ALU.mult).then_inc(setup_v, 1)
            for c in range(CB):
                spread = nc.vector.tensor_scalar(full_g[:, c, 0:P], ident[:], 0.0, bv_c[:, c:c + 1], ALU.mult, ALU.add)
            spread.then_inc(setup_v, 1)
            dve.wait_ge(setup_v, 3)
            nc.vector.tensor_tensor(s2_c, s2_c, s1_c, ALU.mult)
            dve.wait_ge(setup_t, 1)
            nc.vector.tensor_tensor(b_tot[:], pM[:, 0, 0:C], b_tot[:], ALU.add).then_inc(setup_v, 1)

            def weight_bits():
                nc.vector.memset(low[:], 0).then_inc(setup_v, 1)
                dve.wait_ge(setup_v, 5)
                dve.wait_ge(weights_in, 16 * len(FFN))
                done = 5
                for w in FFN:
                    words = w[:].bitcast(I32).rearrange("p k n -> p (k n)")
                    for at in range(0, words.shape[1], LOW_CHUNK):
                        nc.vector.scalar_tensor_tensor(out=low[:], in0=words[:, at:at + LOW_CHUNK], scalar=LOW_BITS,
                                                       in1=low[:], op0=ALU.bitwise_and,
                                                       op1=ALU.bitwise_or).then_inc(setup_v, 1)
                        done += 1
                        dve.wait_ge(setup_v, done)
                nc.vector.tensor_reduce(lowmax[:], low[:], AX_X, ALU.max).then_inc(setup_v, 1)
                dve.wait_ge(setup_t, 2)
                nc.vector.tensor_copy(flag[:], pM[0:1, 0, 0:1]).then_inc(setup_v, 1)

            def work(i, steps):
                for kind, off, a in steps:
                    b = i + off
                    if kind == "max":
                        g, t, p = a
                        n = m_cols(t)
                        nth = b * HEADS + (g * TB + TB - 1 - t) * G + 2 * p
                        need(dve, nt_ready, b * NG + g)
                        for s in range(2):
                            dve.wait_ge(m_ready, nth + s + 1)
                            held(dve)
                            nc.vector.tensor_tensor_reduce(
                                pM[:, s, 0:n], pM[:, s, 0:n], mask[:, T - n:T], 1.0, NEG, ALU.add, ALU.max,
                                mx[:, t, 2 * p + s:2 * p + s + 1]).then_inc(m_done, 1)
                    elif kind == "neg_max":
                        g, = a
                        dve.wait_ge(nm_hi_done, b * NG + g + 1)
                        nc.vector.scalar_tensor_tensor(
                            out=nm[32:NM_ROWS], in0=ring[32:NM_ROWS, BANKS[kind, off, a]], scalar=-1.0,
                            in1=nm[32:NM_ROWS].bitcast(F32),
                            op0=ALU.mult, op1=ALU.subtract).then_inc(nm_lo_done, 1)
                    elif kind == "qk":
                        g, = a
                        dve.wait_ge(qk_hi, b * NG + g + 1)
                        nc.vector.scalar_tensor_tensor(
                            out=c_lo[:], in0=ring[:, BANKS[kind, off, a]], scalar=bqk_c[:, g:g + 1],
                            in1=c_hi[:].bitcast(F32), op0=ALU.add, op1=ALU.subtract).then_inc(qk_lo, 1)
                    elif kind == "x1_turn":
                        c, = a
                        dve.wait_ge(x1_hi, b * CB + c + 1)
                        nc.vector.tensor_tensor(x1Tlo[:, c], ring[:, BANKS[kind, off, a]], x1Thi[:, c].bitcast(F32),
                                                ALU.subtract).then_inc(x1_lo, 1)
                    elif kind == "gu":
                        half, j = a
                        n = b * (2 * KB) + half * KB + j
                        gate, up = (ring[:, BANKS[kind, off, a], m * HALF:(m + 1) * HALF] for m in range(2))
                        dve.wait_ge(tanh_done, n + 1)
                        nc.vector.scalar_tensor_tensor(out=th[:, j % 2], in0=th[:, j % 2], scalar=1.0, in1=up,
                                                       op0=ALU.add, op1=ALU.mult).then_inc(gated, 1)
                        dve.wait_ge(gated, n + 1)
                        need(dve, x_lo, n - 1)
                        nc.vector.scalar_tensor_tensor(out=full_g[:, j % 2], in0=gate,
                                                       scalar=s2_c[:, j:j + 1], in1=th[:, j % 2],
                                                       op0=ALU.mult, op1=ALU.mult).then_inc(ffn_full, 1)
                    elif kind == "h_rest":
                        layer, half, j = a
                        u = u_of(layer, half, j)
                        dve.wait_ge(h_full, b * 32 + u + 1)
                        hi, lo = (Yhi[:, j], Ylo[:, j]) if layer == "h1" else (Xhi[:, j], Xlo[:, j])
                        nc.vector.tensor_tensor(lo, full_h[:, u % 2], hi.bitcast(F32), ALU.subtract).then_inc(h_lo, 1)
                    elif kind == "rec_save":
                        dve.wait_ge(den_in, (b + 1) * 16)
                        need(dve, rec_saved, b * 16)
                        nc.vector.reciprocal(dn[:], dn[:]).then_inc(rc_done, 1)
                    elif kind == "den_turn":
                        for m in range(CB):
                            dve.wait_ge(r_ready, b * CB + m + 1)
                            nc.vector.tensor_tensor(Oc[:, m], Oc[:, m], ring[:, BANKS[kind, off, (m,)]],
                                                    ALU.mult).then_inc(o_norm, 1)
                    elif kind == "y":
                        half, = a
                        rows = xr[:, 2 * half:2 * half + 2]
                        dve.wait_ge(y_ready, b * 2 + half + 1)
                        dve.wait_ge(xr_ready, b + 1)
                        nc.vector.tensor_tensor(rows, ring[:, BANKS[kind, off, a]].rearrange("p (t c) -> p t c", c=C),
                                                rows, ALU.add).then_inc(ln1, 1)
                        dve.wait_ge(ln1, b * LN1 + 2 * half + 1)
                        for t in (2 * half, 2 * half + 1):
                            st = nc.vector.bn_stats(st1[:, t], xr[:, t])
                        st.then_inc(ln1, 1)
                    elif kind == "ln1_stats":
                        dve.wait_ge(ln1, b * LN1 + 4)
                        held(dve)
                        for t in range(TB):
                            mv = nc.vector.bn_aggr(mv1[:, t], st1[:, t])
                        mv.then_inc(ln1, 1)
                        dve.wait_ge(ln1, b * LN1 + 5)
                        nc.vector.tensor_scalar(rs1[:], mv1[:, :, 1], EPS, None, ALU.add).then_inc(ln1, 1)
                    elif kind == "ln1":
                        dve.wait_ge(ln1_pow, b + 1)
                        need(dve, xt_ready, b * CB)
                        need(dve, ln2, (b - 1) * LN2 + 8)
                        for t in range(TB):
                            row = nc.vector.tensor_scalar(x1[:, t], xr[:, t], mv1[:, t, 0:1], rs1[:, t:t + 1],
                                                          ALU.subtract, ALU.mult)
                        row.then_inc(ln1, 1)
                    elif kind == "ffn_out":
                        half, = a
                        at = b * LN2 + 6 * half
                        dve.wait_ge(f_ready, b * 2 + half + 1)
                        need(dve, stored, (b * 2 + half) * 16)
                        for t in range(2):
                            scaled = nc.vector.tensor_tensor(z[:, t], ring[:, BANKS[kind, off, a], t * C:(t + 1) * C],
                                                             s3b[:], ALU.mult)
                        scaled.then_inc(ln2, 1)
                        dve.wait_ge(ln2, at + 1)
                        nc.vector.tensor_tensor(z[:], z[:], x1[:, 2 * half:2 * half + 2], ALU.add).then_inc(ln2, 1)
                    elif kind == "ln2_stats":
                        half, = a
                        at = b * LN2 + 6 * half
                        dve.wait_ge(ln2, at + 2)
                        for t in range(2):
                            st = nc.vector.bn_stats(st2[:, t], z[:, t])
                        st.then_inc(ln2, 1)
                        dve.wait_ge(ln2, at + 3)
                        held(dve)
                        for t in range(2):
                            mv = nc.vector.bn_aggr(mv2[:, t], st2[:, t])
                        mv.then_inc(ln2, 1)
                        dve.wait_ge(ln2, at + 4)
                        nc.vector.tensor_scalar(rs2[:], mv2[:, :, 1], EPS, None, ALU.add).then_inc(ln2, 1)
                    elif kind == "ln2":
                        half, = a
                        dve.wait_ge(ln2_pow, b * 2 + half + 1)
                        for t in range(2):
                            row = nc.vector.tensor_scalar(z[:, t], z[:, t], mv2[:, t, 0:1], rs2[:, t:t + 1],
                                                          ALU.subtract, ALU.mult)
                        row.then_inc(ln2, 1)

            for i in (-1, 0, 1, 2):
                work(i, steps_of(i))
                if i == 0:
                    weight_bits()
            with dve.Fori(3, B - 1) as i:
                work(i, steps_of(None))
            for i in (B - 1, B, B + 1):
                work(i, steps_of(i))

        @block.tensor
        def _(pe):
            RELEASE = {
                "qk": lambda g: (qk_lo, NG, g + 1),
                "v": lambda kt: (v_copied, TB, kt + 1),
                "gu": lambda half, j: (ffn_full, 2 * KB, half * KB + j + 1),
                "h1": lambda half, j: (h_full, 32, u_of("h1", half, j) + 1),
                "h2": lambda half, j: (h_full, 32, u_of("h2", half, j) + 1),
                "ffn_out": lambda half: (ln2, LN2, 6 * half + 1),
                "y": lambda half: (ln1, LN1, 2 * half + 1),
                "x1_turn": lambda c: (x1_lo, CB, c + 1),
                "neg_max": lambda g: (nm_lo_done, NG, g + 1),
                "den_turn": lambda m: (o_norm, CB, m + 1),
            }

            def iteration(i, steps, taken, general):

                def bank(kind, off, a):
                    n = BANKS[kind, off, a]
                    if n in taken:
                        last, last_off, last_a = taken[n]
                        s, per, nth = RELEASE[last](*last_a)
                        pe.wait_ge(s, (i + last_off) * per + nth)
                    taken[n] = (kind, off, a)
                    return ring[:, n]

                def parts(w, act):
                    return (w.bitcast(F32), act.bitcast(F32)) if general else (w, act)

                for kind, off, a in steps:
                    b = i + off
                    if kind == "exp":
                        g, kt, p = a
                        n, slot = e_cols(kt), g % 2
                        if kt == 0 and p == 0:
                            pe.wait_ge(nm_in, (b * NG + g + 1) * 64)
                        for s in range(2):
                            need(pe, exp_done, b * HEADS + 2 * e_of(g, kt, p) + s - 1)
                            rows = slice(SROWS * s, SROWS * (s + 1))
                            nc.tensor.matmul(pS[:, s, 0:n], Ks[rows, slot, p, kt * P:(kt + 1) * P],
                                             Qs[rows, slot, p, kt * P:T], start=True, stop=True).then_inc(e_ready, 1)
                    elif kind == "max":
                        g, t, p = a
                        n, slot = m_cols(t), g % 2
                        nth = b * HEADS + (g * TB + TB - 1 - t) * G + 2 * p
                        if t == TB - 1 and p == 0:
                            pe.wait_ge(stack_in[slot], (b * 2 + g // 2 + 1) * 32)
                        for s in range(2):
                            need(pe, m_done, nth + s - 1)
                            rows = slice(SROWS * s, SROWS * (s + 1))
                            nc.tensor.matmul(pM[:, s, 0:n], Qs[rows, slot, p, t * P:(t + 1) * P],
                                             Ks[rows, slot, p, 0:n], start=True, stop=True).then_inc(m_ready, 1)
                    elif kind == "neg_max":
                        g, = a
                        pe.wait_ge(m_done, b * HEADS + (g + 1) * TB * G)
                        to = bank(kind, off, a)
                        for t in range(TB):
                            for at in (0, 32):
                                mm = nc.tensor.matmul(to[at:at + G, t * P:(t + 1) * P], mx[:, t], ident[:],
                                                      start=True, stop=True)
                        mm.then_inc(nt_ready, 1)
                    elif kind == "pv":
                        g, kt = a
                        n = e_cols(kt)
                        if kt == 0:
                            if g == 0:
                                pe.wait_ge(v_copied, (b + 1) * TB)
                            need(pe, o_out, b * NG + g)
                        pe.wait_ge(mask_done, b * (NG * TB * PAIRS) + e_of(g, kt, PAIRS - 1) + 1)
                        for p in range(PAIRS):
                            for s in range(2):
                                j = 2 * p + s
                                mm = nc.tensor.matmul(pO[32 * j:32 * j + VW, kt * P:T], Vo[:, kt, G * g + j],
                                                      probs[:, e_of(g, kt, p) % NP_BUF, s, 0:n],
                                                      start=(kt == 0), stop=(kt == TB - 1))
                        mm.then_inc(pv_done, 1)
                    elif kind == "qk":
                        g, = a
                        pe.wait_ge(xT_in, (b + 1) * 16)
                        to = bank(kind, off, a)
                        for c in range(CB):
                            mm = nc.tensor.matmul(to, Wqk[:, c, g], xTs[:, c], start=(c == 0), stop=(c == CB - 1))
                        mm.then_inc(qk_ready, 1)
                    elif kind == "v":
                        kt, = a
                        to = bank(kind, off, a)
                        for c in range(CB):
                            mm = nc.tensor.matmul(to[:, 0:C], xTs[:, c, kt * P:(kt + 1) * P], Wv[:, c],
                                                  start=(c == 0), stop=(c == CB - 1))
                        mm.then_inc(v_ready, 1)
                    elif kind == "den_turn":
                        pe.wait_ge(rec_in, (b + 1) * 16)
                        for m in range(CB):
                            to = bank(kind, off, (m,))
                            nc.tensor.matmul(to, sel[:, m], Osb[0:H], start=True, stop=True).then_inc(r_ready, 1)
                    elif kind == "y":
                        half, = a
                        pe.wait_ge(o_norm, (b + 1) * CB)
                        to = bank(kind, off, a)
                        for t in range(2):
                            tok = slice((2 * half + t) * P, (2 * half + t + 1) * P)
                            for c in range(CB):
                                mm = nc.tensor.matmul(to[:, t * C:(t + 1) * C], Oc[:, c, tok], Wout[:, c],
                                                      start=(c == 0), stop=(c == CB - 1))
                        mm.then_inc(y_ready, 1)
                    elif kind == "x1_turn":
                        c, = a
                        pe.wait_ge(ln1, (b + 1) * LN1)
                        to = bank(kind, off, a)
                        for t in range(TB):
                            mm = nc.tensor.transpose(to[:, t * P:(t + 1) * P], x1[:, t, c * P:(c + 1) * P], ident[:])
                        mm.then_inc(xt_ready, 1)
                    elif kind == "gu":
                        half, j = a
                        pe.wait_ge(x1_lo, (b + 1) * CB)
                        tok = slice(half * HALF, (half + 1) * HALF)
                        to = bank(kind, off, a)
                        for n, W in enumerate((W1, W2)):
                            for c in range(CB):
                                for X in (x1Thi, x1Tlo):
                                    w, x_part = parts(W[:, c, j * P:(j + 1) * P], X[:, c, tok])
                                    mm = nc.tensor.matmul(to[:, n * HALF:(n + 1) * HALF], w, x_part,
                                                          start=(c == 0 and X is x1Thi),
                                                          stop=(c == CB - 1 and X is x1Tlo))
                        mm.then_inc(gu_ready, 1)
                    elif kind in ("h1", "h2"):
                        half, j = a
                        W, src = (H1, (Xhi, Xlo)) if kind == "h1" else (H2, (Yhi, Ylo))
                        s, n = (x_lo, b * (2 * KB) + (half + 1) * KB) if kind == "h1" else (h_lo, b * 32 + half * 16 + KB)
                        to = bank(kind, off, a)[:, 0:HALF]
                        for k in range(KB):
                            if j == 0 and k in (0, KB - 1):
                                pe.wait_ge(s, n - (k == 0))
                            for m, X in enumerate(src):
                                w, x_part = parts(W[:, k, j * P:(j + 1) * P], X[:, k])
                                mm = nc.tensor.matmul(to, w, x_part, start=(k == 0 and m == 0),
                                                      stop=(k == KB - 1 and m == 1))
                        mm.then_inc(h_ready, 1)
                    elif kind == "ffn_out":
                        half, = a
                        to = bank(kind, off, a)
                        for t in range(2):
                            tok = slice(t * P, (t + 1) * P)
                            for k in range(KB):
                                if t == 0 and k in (0, KB - 1):
                                    pe.wait_ge(h_lo, b * 32 + half * 16 + 2 * KB - (k == 0))
                                for m, X in enumerate((Xhi, Xlo)):
                                    w, x_part = parts(W3[:, k], X[:, k, tok])
                                    mm = nc.tensor.matmul(to[:, t * C:(t + 1) * C], x_part, w,
                                                          start=(k == 0 and m == 0), stop=(k == KB - 1 and m == 1))
                        mm.then_inc(f_ready, 1)
                for n, (kind, off, a) in taken.items():
                    taken[n] = (kind, off - 1, a)

            def ffn_iterations(taken, general):
                for i in (1, 2):
                    iteration(i, steps_of(i), taken, general)
                with pe.Fori(3, B - 1) as i:
                    iteration(i, steps_of(None), taken, general)
                for i in (B - 1, B, B + 1):
                    iteration(i, steps_of(i), taken, general)

            pe.wait_ge(params_in, 16 * N_PARAMS)
            pe.wait_ge(setup_v, 3)
            for c in range(CB):
                mm = nc.tensor.matmul(pM[:, 0, 0:C], full_g[:, c, 0:P], Wout[:, c], start=(c == 0), stop=(c == CB - 1))
            mm.then_inc(setup_t, 1)
            pe.wait_ge(setup_v, 4)
            taken = {}
            for i in (-1, 0):
                iteration(i, steps_of(i), taken, False)
            chunks = sum(w.shape[1] * w.shape[2] // LOW_CHUNK for w in FFN)
            pe.wait_ge(setup_v, 5 + chunks + 1)
            nc.tensor.matmul(pM[0:1, 0, 0:1], lowmax[:], ones_c[:], start=True, stop=True).then_inc(setup_t, 1)
            pe.wait_ge(setup_v, 5 + chunks + 2)
            has_low_bits = pe.value_load(flag[0:1, 0:1], min_val=0, max_val=1 << 20)
            with pe.If(has_low_bits > 0):
                ffn_iterations(dict(taken), True)
            with pe.Else():
                ffn_iterations(dict(taken), False)


def kernel(**inputs):
    import concourse.bacc as bacc
    from concourse.bass_utils import run_bass_kernel_spmd

    a = {k: np.asarray(v) for k, v in inputs.items()}
    x = a["L0_attn_x"]
    w_qkv, b_qkv = a["L0_attn_Wqkv"], a["L0_attn_bqkv"]
    w_qk = np.ascontiguousarray(w_qkv[:, :2 * C].reshape(C, 2, NG, G * D).transpose(0, 2, 1, 3)).reshape(C, NG, P)
    b_qk = b_qkv[:2 * C].reshape(2, NG, G * D).transpose(1, 0, 2).reshape(NG, P)
    cols = np.zeros((P, 40), np.float32)
    cols[:, 0:4] = b_qk.T
    cols[:, 4:6] = b_qkv[2 * C:].reshape(CB, P).T
    for n, name in enumerate(("w1_s", "w2_s", "h1_s", "h2_s")):
        cols[:, 8 * n + 8:8 * n + 16] = a["L0_ffn_" + name].reshape(KB, P).T
    arrays = {
        "x": np.ascontiguousarray(x),
        "xT": np.ascontiguousarray(x.transpose(0, 2, 1)),
        "w_qk": w_qk,
        "w_v": np.ascontiguousarray(w_qkv[:, 2 * C:]),
        "w_out": np.ascontiguousarray(a["L0_attn_Wout"]),
    }
    for name in ("w1", "w2", "h1", "h2", "w3"):
        arrays[name] = np.ascontiguousarray(a[f"L0_ffn_{name}_w"].T)
    arrays["cols"] = cols
    arrays["b_out"] = np.ascontiguousarray(a["L0_attn_bout"])
    arrays["s3"] = np.ascontiguousarray(a["L0_ffn_w3_s"])

    nc = bacc.Bacc("TRN2", target_bir_lowering=False, num_devices=1)
    args = {n: nc.dram_tensor(f"in_{n}", v.shape, F32, kind="ExternalInput").ap() for n, v in arrays.items()}
    out = nc.dram_tensor("out_0", (B, T, C), F32, kind="ExternalOutput").ap()
    build(nc, args["x"], args["xT"], args["w_qk"], args["w_v"], args["w_out"],
          [args[n] for n in ("w1", "w2", "h1", "h2", "w3")], args["cols"], args["b_out"], args["s3"], out)
    got = run_bass_kernel_spmd(nc, [{f"in_{n}": v for n, v in arrays.items()}], core_ids=[0])
    return got.results[0]["out_0"]
```

```python
from contextlib import ExitStack

import numpy as np

import concourse.bass as bass
from concourse import mybir

F32 = mybir.dt.float32
F32R = mybir.dt.float32r
BF16 = mybir.dt.bfloat16
I32 = mybir.dt.int32
ACT = mybir.ActivationFunctionType
ALU = mybir.AluOpType
AX_X = mybir.AxisListType.X

P = 128
B, T, C = 16, 512, 256
H = 16
D = C // H
HID = 1024
SCALE = float(D) ** -0.5
EPS = 1e-5
NEG = -3.0e38
PIECE = 2048
LOW_BITS = 0xFFF

CB = C // P
KB = HID // P
TB = T // P
HALF = T // 2
G = 4
NG = H // G
PAIRS = G // 2
PARTS = 4
SROWS = PARTS * D
NM_ROWS = 32 + G
VW = D + 1
NP_BUF = 4
MISC = 3


def plan_iteration():
    steps = []

    def add(kind, off, *args):
        steps.append((kind, off, args))

    def exps(g, between):
        e = 0
        for kt in range(TB):
            for p in range(PAIRS):
                add("exp", 0, g, kt, p)
                steps.extend(between.get(e, []))
                e += 1
            if kt:
                add("pv", 0, g, kt - 1)

    def last_pv(g):
        add("pv", 0, g, TB - 1)
        add("o_out", 0, g)
        add("stack", 0 if g + 2 < NG else 1, (g + 2) % NG)

    def hidden(layer, off, half, g, early, after):
        if not early:
            last_pv(g)
            steps.extend(after.get(-1, []))
        for j in range(early, KB):
            add(layer, off, half, j)
            waiting = [(layer, half, k) for k in range(early)] if j == early else []
            for k, unit in enumerate(waiting):
                steps.append(("h_act", off, unit))
                if k == 0:
                    last_pv(g)
            if waiting:
                steps.append(("h_rest", off, waiting.pop(0)))
            add("h_act", off, layer, half, j)
            steps.extend(after.get(j, []))
            steps.extend(("h_rest", off, unit) for unit in waiting)
            add("h_rest", off, layer, half, j)

    def maxes(off, g):
        return [("max", off, (g, t, p)) for t in reversed(range(TB)) for p in range(PAIRS)]

    def gated(off, half, at, others):
        between = {e: list(more) for e, more in others.items()}
        for e, n in at:
            between.setdefault(e, []).append(("gu", off, (half, n)))
            if n:
                between.setdefault(e + (e == 6 and n == KB - 1), []).append(("ffn_hi", off, (half, n - 1)))
        return between

    m = maxes(0, 1)
    add("table", 0, "Exp", 0)
    exps(0, {0: [("y", -1, (0,)), m[0]], 1: [("y", -1, (1,))], 2: [("h2", -2, (1, 0))],
             4: [m[1]], 5: [m[2]], 6: [("h2", -2, (1, 1))], 7: [("ln1_stats", -1, ()), m[3]]})
    add("table", 0, "Gelu", 1)
    hidden("h2", -2, 1, 0, 2, {2: [m[4]], 3: [m[5]], 4: [m[6]], 5: [m[7]], 6: [("neg_max", 0, (1,))]})
    add("table", 0, "Exp", 2)
    add("ffn_out", -2, 1)
    m = maxes(0, 2)
    add("ln1", -1)
    exps(1, gated(-1, 0, [(4, 0), (4, 1), (5, 2), (5, 3), (6, 4), (6, 5), (7, 6), (7, 7)],
                  {0: [("qk", 0, (3,)), ("load_xT", 1, ()), m[0]], 1: [("x1_turn", -1, (0,))],
                   2: [("x1_turn", -1, (1,))], 3: [m[1]], 5: [m[2]]}))
    steps.append(m[3])
    add("ffn_hi", -1, 0, KB - 1)
    add("table", 0, "Gelu", 3)
    hidden("h1", -1, 0, 1, 0, {0: [m[4]], 1: [m[5]], 2: [m[6], ("load_x", 0, ())], 3: [m[7]],
                               4: [("neg_max", 0, (2,))], 5: [("ln2_stats", -2, (1,))], 6: [("ln2", -2, (1,))]})
    m = maxes(0, 3)
    add("table", 0, "Exp", 4)
    add("qk", 1, 0)
    exps(2, {0: [("h2", -1, (0, 0))], 1: [m[0]], 2: [("h2", -1, (0, 1))], 3: [m[1]], 4: [m[2]], 6: [m[3]]})
    add("table", 0, "Gelu", 5)
    hidden("h2", -1, 0, 2, 2, {2: [m[4]], 3: [m[5]], 4: [m[6]], 5: [m[7]], 6: [("neg_max", 0, (3,))]})
    add("table", 0, "Exp", 6)
    add("qk", 1, 1)
    add("ffn_out", -1, 0)
    m = maxes(1, 0)
    add("gu", -1, 1, 0)
    exps(3, gated(-1, 1, [(0, 1), (1, 2), (2, 3), (3, 4), (4, 5), (5, 6), (6, 7)],
                  {1: [m[0]]}))
    steps.append(m[1])
    add("ffn_hi", -1, 1, KB - 1)
    add("table", 0, "Gelu", 7)
    hidden("h1", -1, 1, 3, 0, {-1: [("v", 1, (0,)), m[2]], 0: [m[3], ("v", 1, (1,)), ("den", 0, ())],
                               1: [m[4], ("v", 1, (2,))], 2: [m[5], ("v", 1, (3,))], 3: [m[6], ("rec_save", 0, ())],
                               4: [m[7], ("rec_load", 0, ())], 5: [("neg_max", 1, (0,)), ("qk", 1, (2,))],
                               6: [("ln2_stats", -1, (0,)), ("den_turn", 0, ())], 7: [("ln2", -1, (0,))]})
    return steps


STEPS = plan_iteration()
BANKED = [s for s in STEPS if s[0] in
          ("qk", "v", "gu", "h1", "h2", "ffn_out", "y", "x1_turn", "neg_max")]


def ring_banks():
    at, banks = 0, {}
    for kind, off, args in STEPS:
        n = 2 if kind == "den_turn" else 1 if (kind, off, args) in BANKED else 0
        for m in range(n):
            key = (kind, off, args + (m,)) if kind == "den_turn" else (kind, off, args)
            banks[key] = at % MISC
            at += 1
    return banks


BANKS = ring_banks()


def steps_of(i):
    return [s for s in STEPS if i is None or 0 <= i + s[1] < B]


def over(nc, base, name, shape, dt):
    return nc.alloc_sbuf_tensor_at(name, shape, dt, offset=base)


def build(nc, x, xT, w_qk, w_v, w_out, w_ffn, cols_in, b_out, s3, out):
    with ExitStack() as ctx:
        def sb(name, shape, dt=F32):
            return ctx.enter_context(nc.sbuf_tensor(name, shape, dt))

        def psum(name, shape):
            return ctx.enter_context(nc.psum_tensor(name, shape, F32))

        def sem(name):
            return ctx.enter_context(nc.semaphore(name))

        def dram(name, shape):
            return nc.dram_tensor(name, shape, F32, kind="Internal").ap()

        W1 = sb("W1", [P, CB, HID], F32R)
        W2 = sb("W2", [P, CB, HID], F32R)
        H1 = sb("H1", [P, KB, HID], F32R)
        H2 = sb("H2", [P, KB, HID], F32R)
        W3 = sb("W3", [P, KB, C], F32R)
        FFN = (W1, W2, H1, H2, W3)
        Wqk = sb("Wqk", [P, CB, NG, P])
        Wv = sb("Wv", [P, CB, C])
        Wout = sb("Wout", [P, CB, C])
        Qs = sb("Qs", [P, 2, PAIRS, T], F32R)
        Ks = sb("Ks", [P, 2, PAIRS, T], F32R)
        Vo = sb("Vo", [P, TB, H, VW])
        o_at = nc.sbuf_base
        Osb = sb("Osb", [P, T])
        th = over(nc, o_at, "th", [P, 2, HALF], F32)
        rec = over(nc, o_at, "rec", [2 * H, T], F32R)
        Oc = sb("Oc", [P, CB, T])
        low_at = nc.sbuf_base
        Xhi = sb("Xhi", [P, KB, HALF], F32R)
        low = over(nc, low_at, "low_bits", [P, PIECE], I32)
        Xlo = sb("Xlo", [P, KB, HALF], F32R)
        Yhi = sb("Yhi", [P, KB, HALF], F32R)
        Ylo = sb("Ylo", [P, KB, HALF], F32R)
        x1Thi = sb("x1Thi", [P, CB, T], F32R)
        x1Tlo = sb("x1Tlo", [P, CB, T], F32R)
        g_at = nc.sbuf_base
        full_g = sb("full_g", [P, 2, HALF])
        dn = over(nc, g_at, "dn", [P, H * T // P], F32)
        full_h = sb("full_h", [P, 2, HALF])
        xr = sb("xr", [P, TB, C])
        x1 = sb("x1", [P, TB, C])
        z = sb("z", [P, 2, C])
        probs = sb("probs", [P, NP_BUF, 2, T])
        c_hi = sb("c_hi", [P, T], F32R)
        c_lo = sb("c_lo", [P, T], F32R)
        xTs = sb("xTs", [P, CB, T])
        nm = sb("nm", [NM_ROWS, T], F32R)
        mask = sb("mask", [P, T], BF16)
        ident = sb("ident", [P, P])
        sel = sb("sel", [2 * H, CB, P], F32R)
        b_tot = sb("b_tot", [P, C])
        s3b = sb("s3b", [P, C])
        cols = sb("cols", [P, 40])
        bqk_c, bv_c = cols[:, 0:NG], cols[:, 4:6]
        s1_c, s2_c, sh1_c, sh2_c = (cols[:, 8 * n:8 * n + 8] for n in (1, 2, 3, 4))
        mx = sb("mx", [P, TB, G])
        rc = sb("rc", [P, 2, H * T // P], F32R)
        st1, mv1, rs1 = sb("st1", [P, TB, 6]), sb("mv1", [P, TB, 2]), sb("rs1", [P, TB])
        st2, mv2, rs2 = sb("st2", [P, 2, 6]), sb("mv2", [P, 2, 2]), sb("rs2", [P, 2])
        small = sb("small", [P, TB + 2])
        minus_half, lowmax, ones_c = small[:, 0:TB], small[:, TB:TB + 1], small[:, TB + 1:TB + 2]
        loaded = sb("loaded", [1, 1])
        flag = sb("flag", [1, 1], I32)

        pS = psum("pS", [P, 2, T])
        pM = psum("pM", [P, 2, T])
        pO = psum("pO", [P, T])
        ring = psum("ring", [P, MISC, T])

        raw = [dram(f"raw{n}", w.shape) for n, w in enumerate(w_ffn)]
        qk_d = dram("qk_d", [NG, P, PARTS, T])
        den_d = dram("den_d", [H, T])
        rec_d = dram("rec_d", [2, H, T])

        xT_in, x_in, params_in, raw_in = map(sem, ("xT_in", "x_in", "params_in", "raw_in"))
        weights_in = [sem(f"weights_in{n}") for n in range(len(FFN))]
        const_rows, osb_set = sem("const_rows"), sem("osb_set")
        qk_saved, nm_in, o_moved = map(sem, ("qk_saved", "nm_in", "o_moved"))
        stack_in = [sem("stack_in0"), sem("stack_in1")]
        den_in, rec_saved, rec_in, stored = map(sem, ("den_in", "rec_saved", "rec_in", "stored"))
        qk_ready, v_ready, e_ready, m_ready, pv_done = map(sem, ("qk_ready", "v_ready", "e_ready", "m_ready", "pv_done"))
        nt_ready, xt_ready, gu_ready, h_ready = map(sem, ("nt_ready", "xt_ready", "gu_ready", "h_ready"))
        f_ready, y_ready, r_ready = map(sem, ("f_ready", "y_ready", "r_ready"))
        qk_hi, exp_done, tanh_done, x_hi, h_full = map(sem, ("qk_hi", "exp_done", "tanh_done", "x_hi", "h_full"))
        o_out, nm_hi_done, x1_hi, v_copied = map(sem, ("o_out", "nm_hi_done", "x1_hi", "v_copied"))
        qk_lo, m_done, nm_lo_done, gated, ffn_full, h_lo = map(sem, ("qk_lo", "m_done", "nm_lo_done", "gated", "ffn_full", "h_lo"))
        x1_lo, rc_done, o_norm, ln1, ln2 = map(sem, ("x1_lo", "rc_done", "o_norm", "ln1", "ln2"))
        mask_done, x_lo, xr_ready, ln1_pow, ln2_pow = map(sem, ("mask_done", "x_lo", "xr_ready", "ln1_pow", "ln2_pow"))
        consts, setup_v, setup_t, passed = map(sem, ("consts", "setup_v", "setup_t", "passed"))
        tables = sem("tables")

        LN1, LN2 = 7, 12
        TABLES = sum(kind == "table" for kind, _, _ in STEPS)
        N_PARAMS = 6
        SAVES = 16 * 5
        N_CONSTS = 10

        def need(eng, s, n):
            if not (isinstance(n, int) and n <= 0):
                eng.wait_ge(s, n)

        def held(eng):
            eng.sem_inc(passed, 1)

        def pipeline(eng, body):
            for i in (-1, 0, 1, 2):
                body(i, steps_of(i))
            with eng.Fori(3, B - 1) as i:
                body(i, steps_of(None))
            for i in (B - 1, B, B + 1):
                body(i, steps_of(i))

        def e_of(g, kt, p):
            return (g * TB + kt) * PAIRS + p

        HEADS = NG * TB * G

        def u_of(kind, half, j):
            return (2 * half + (kind == "h2")) * KB + j

        def e_cols(kt):
            return T - kt * P

        def m_cols(t):
            return (t + 1) * P

        block = ctx.enter_context(nc.Block())

        @block.sync
        def _(sp):
            sp.dma_start(Wqk[:], w_qk.rearrange("(c p) g n -> p c g n", p=P)).then_inc(params_in, 16)
            sp.dma_start(cols[:], cols_in).then_inc(params_in, 16)
            sp.dma_start(xTs[:], xT[0].rearrange("(c p) t -> p c t", p=P)).then_inc(xT_in, 16)
            sp.wait_ge(osb_set, 2)
            for g in range(NG):
                sp.dma_start(qk_d[g, :, PARTS - 1], Osb[:]).then_inc(const_rows, 16)
            sp.dma_start(Wv[:], w_v.rearrange("(c p) n -> p c n", p=P)).then_inc(params_in, 16)
            sp.dma_start(Wout[:], w_out.rearrange("(c p) n -> p c n", p=P)).then_inc(params_in, 16)
            sp.dma_start(b_tot[:], b_out.rearrange("(a n) -> a n", a=1).broadcast_to([P, C])).then_inc(params_in, 16)
            sp.dma_start(s3b[:], s3.rearrange("(a n) -> a n", a=1).broadcast_to([P, C])).then_inc(params_in, 16)

            pieces = [(n, k) for n, w in enumerate(FFN) for k in range(0, w.shape[1], PIECE // w.shape[2])]
            weight_moves = [(True, p) for p in pieces] + [(False, p) for p in pieces]

            def move_piece():
                to_scratch, (n, k) = weight_moves.pop(0)
                blocks = PIECE // FFN[n].shape[2]
                rows = slice(k * P, (k + blocks) * P)
                if to_scratch:
                    sp.dma_start(raw[n][rows], w_ffn[n][rows]).then_inc(raw_in, 16)
                else:
                    sp.wait_ge(raw_in, 16 * len(pieces))
                    sp.dma_start(FFN[n][:, k:k + blocks].bitcast(F32),
                                 raw[n][rows].rearrange("(k p) n -> p k n", p=P)).then_inc(weights_in[n], 16)

            def move(i, steps):
                for kind, off, a in steps:
                    b = i + off
                    if kind == "load_xT" and not (isinstance(b, int) and b == 0):
                        sp.wait_ge(qk_ready, b * NG)
                        held(sp)
                        sp.dma_start(xTs[:], xT[bass.ds(b, 1)].rearrange("a (c p) t -> p (a c) t", p=P)).then_inc(xT_in, 16)
                    elif kind == "load_x":
                        need(sp, ln1, b * LN1)
                        held(sp)
                        sp.dma_start(xr[:], x[bass.ds(b, 1)].rearrange("a (t p) c -> p (a t) c", p=P)).then_inc(x_in, 16)
                    elif kind == "qk":
                        g, = a
                        sp.wait_ge(qk_lo, b * NG + g + 1)
                        for part, src, rows in ((0, c_hi, slice(0, P)), (1, c_hi, slice(0, G * D)), (1, c_lo, slice(G * D, P)),
                                                (2, c_lo, slice(0, G * D)), (2, c_hi, slice(G * D, P))):
                            sp.dma_start(qk_d[g, rows, part], src[rows].bitcast(F32)).then_inc(qk_saved, 16)
                    elif kind == "stack":
                        g, = a
                        slot = g % 2
                        sp.wait_ge(qk_saved, (b * NG + g + 1) * SAVES)
                        held(sp)
                        need(sp, e_ready, b * HEADS + (g - 1) * TB * G)
                        if g < 2 and isinstance(b, int) and b == 0:
                            sp.wait_ge(const_rows, 16 * NG)
                        held(sp)
                        for dst, qk in ((Qs, 0), (Ks, 1)):
                            rows = qk_d[g, qk * G * D:(qk + 1) * G * D].rearrange("(p s d) r n -> (s d r) p n", p=PAIRS, s=2)
                            sp.dma_start(dst[:, slot].bitcast(F32), rows).then_inc(stack_in[slot], 16)
                    elif kind == "neg_max":
                        g, = a
                        sp.wait_ge(nm_lo_done, b * NG + g + 1)
                        for j in range(G):
                            at = 64 * (j % 2) + PARTS - 1
                            sp.dma_start(Qs[at:at + PARTS + 1:PARTS, g % 2, j // 2].bitcast(F32),
                                         nm[j:NM_ROWS:32].bitcast(F32)).then_inc(nm_in, 16)
                        for _ in range(min(6, len(weight_moves))):
                            move_piece()
                    elif kind == "o_out":
                        g, = a
                        sp.wait_ge(o_out, b * NG + g + 1)
                        held(sp)
                        if g == 0:
                            need(sp, y_ready, b * 2)
                        held(sp)
                        for j in range(G):
                            at = 64 * (g % 2) + D * j
                            sp.dma_start(Oc[at:at + D, g // 2], Osb[32 * j:32 * j + D]).then_inc(o_moved, 16)
                        sp.dma_start(den_d[g * G:(g + 1) * G], Osb[D:P:32, :]).then_inc(o_moved, 16)
                    elif kind == "den":
                        need(sp, x_lo, b * (2 * KB))
                        held(sp)
                        sp.wait_ge(o_moved, (b + 1) * (NG * 80))
                        sp.dma_start(dn[:], den_d.rearrange("h (c n) -> (h c) n", n=H * T // P)).then_inc(den_in, 16)
                    elif kind == "rec_save":
                        sp.wait_ge(rc_done, (b + 1) * 3)
                        sp.dma_start(rec_d.rearrange("a h (c n) -> (h c) a n", n=H * T // P), rc[:].bitcast(F32)).then_inc(rec_saved, 16)
                    elif kind == "rec_load":
                        sp.wait_ge(rec_saved, (b + 1) * 16)
                        sp.dma_start(rec[:].bitcast(F32), rec_d.rearrange("a h n -> (a h) n")).then_inc(rec_in, 16)
                    elif kind == "ln2":
                        half, = a
                        sp.wait_ge(ln2, b * LN2 + 6 * half + 6)
                        held(sp)
                        sp.dma_start(out[bass.ds(b, 1)].rearrange("a (t p) c -> p (a t) c", p=P)[:, 2 * half:2 * half + 2],
                                     z[:]).then_inc(stored, 16)

            for i in (-1, 0, 1, 2):
                move(i, steps_of(i))
            with sp.Fori(3, B - 1) as i:
                move(i, steps_of(None))
            for i in (B - 1, B, B + 1):
                move(i, steps_of(i))
            sp.wait_ge(stored, B * 32)

        @block.gpsimd
        def _(pool):
            nc.gpsimd.memset(ident[:], 0.0).then_inc(consts, 1)
            nc.gpsimd.memset(mask[:], 0.0).then_inc(consts, 1)
            heads = probs[0:2 * H, 0, 0, 0:C].rearrange("h (e d) -> h e d", d=D)
            nc.gpsimd.memset(probs[0:2 * H, 0, 0, 0:C], 0.0).then_inc(consts, 1)
            nc.gpsimd.memset(minus_half, -0.5).then_inc(consts, 1)
            nc.gpsimd.memset(ones_c, 1.0).then_inc(consts, 1)
            nc.gpsimd.memset(Vo[:], 1.0).then_inc(consts, 1)
            pool.wait_ge(consts, 6)
            nc.gpsimd.affine_select(out=ident[:], in_=ident[:], compare_op=ALU.not_equal, fill=1.0, base=0,
                                    pattern=[[-1, P]], channel_multiplier=1).then_inc(consts, 1)
            tri = mask[:, T - P:T]
            nc.gpsimd.affine_select(out=tri, in_=tri, compare_op=ALU.is_ge, fill=NEG, base=0,
                                    pattern=[[-1, P]], channel_multiplier=1).then_inc(consts, 1)
            for n in range(2):
                pool.wait_ge(consts, 8 + n)
                nc.gpsimd.affine_select(out=heads, in_=heads, compare_op=ALU.not_equal, fill=1.0, base=-n * H,
                                        pattern=[[-1, H], [0, D]], channel_multiplier=1).then_inc(consts, 1)

            def work(i, steps):
                for kind, off, a in steps:
                    b = i + off
                    if kind == "exp":
                        g, kt, p = a
                        e = e_of(g, kt, p)
                        pool.wait_ge(exp_done, b * HEADS + 2 * e + 2)
                        held(pool)
                        tri_p = probs[:, e % NP_BUF, :, 0:P]
                        nc.gpsimd.affine_select(out=tri_p, in_=tri_p, compare_op=ALU.is_ge, fill=0.0, base=0,
                                                pattern=[[0, 2], [1, P]], channel_multiplier=-1).then_inc(mask_done, 1)
                    elif kind == "ffn_hi":
                        half, j = a
                        pool.wait_ge(x_hi, b * (2 * KB) + half * KB + j + 1)
                        nc.gpsimd.tensor_tensor(Xlo[:, j], full_g[:, j % 2], Xhi[:, j].bitcast(F32),
                                                ALU.subtract).then_inc(x_lo, 1)
                    elif kind == "load_x":
                        if isinstance(b, int) and b == 0:
                            pool.wait_ge(setup_v, 4)
                        pool.wait_ge(x_in, (b + 1) * 16)
                        for t in range(TB):
                            add_b = nc.gpsimd.tensor_tensor(xr[:, t], xr[:, t], b_tot[:], ALU.add)
                        add_b.then_inc(xr_ready, 1)
                    elif kind == "ln1_stats":
                        pool.wait_ge(ln1, b * LN1 + 6)
                        nc.gpsimd.tensor_tensor(rs1[:], rs1[:], minus_half, ALU.pow).then_inc(ln1_pow, 1)
                    elif kind == "ln2":
                        half, = a
                        pool.wait_ge(ln2, b * LN2 + 6 * half + 5)
                        nc.gpsimd.tensor_tensor(rs2[:], rs2[:], minus_half[:, 0:2], ALU.pow).then_inc(ln2_pow, 1)

            pipeline(pool, work)

        @block.scalar
        def _(act):
            act.wait_ge(consts, 5)

            def work(i, steps):
                for kind, off, a in steps:
                    b = i + off
                    if kind == "exp":
                        g, kt, p = a
                        e, n = e_of(g, kt, p), e_cols(kt)
                        need(act, pv_done, b * (NG * TB) + g * TB + kt - 1)
                        for s in range(2):
                            act.wait_ge(e_ready, b * HEADS + 2 * e + s + 1)
                            nc.scalar.activation(probs[:, e % NP_BUF, s, 0:n], pS[:, s, 0:n], ACT.Exp,
                                                 scale=SCALE).then_inc(exp_done, 1)
                    elif kind == "neg_max":
                        g, = a
                        act.wait_ge(nt_ready, b * NG + g + 1)
                        need(act, nm_in, (b * NG + g) * 64)
                        nc.scalar.activation(nm[:], ring[0:NM_ROWS, BANKS[kind, off, a]], ACT.Identity,
                                             scale=-1.0).then_inc(nm_hi_done, 1)
                    elif kind == "qk":
                        g, = a
                        act.wait_ge(qk_ready, b * NG + g + 1)
                        need(act, qk_saved, (b * NG + g) * SAVES)
                        nc.scalar.activation(c_hi[:], ring[:, BANKS[kind, off, a]], ACT.Identity,
                                             bias=bqk_c[:, g:g + 1]).then_inc(qk_hi, 1)
                    elif kind == "v":
                        kt, = a
                        act.wait_ge(v_ready, b * TB + kt + 1)
                        need(act, pv_done, b * (NG * TB))
                        if isinstance(b, int) and b == 0:
                            act.wait_ge(consts, N_CONSTS)
                        nc.scalar.activation(
                            Vo[:, kt, :, 0:D], ring[:, BANKS[kind, off, a], 0:C].rearrange("p (h d) -> p h d", d=D),
                            ACT.Copy).then_inc(v_copied, 1)
                    elif kind == "o_out":
                        g, = a
                        act.wait_ge(pv_done, b * (NG * TB) + (g + 1) * TB)
                        need(act, o_moved, (b * NG + g) * 80)
                        if g == 0:
                            need(act, r_ready, b * CB)
                        nc.scalar.activation(Osb[:], pO[:], ACT.Copy).then_inc(o_out, 1)
                    elif kind == "x1_turn":
                        c, = a
                        act.wait_ge(xt_ready, b * CB + c + 1)
                        need(act, gu_ready, b * (2 * KB))
                        nc.scalar.activation(x1Thi[:, c], ring[:, BANKS[kind, off, a]], ACT.Copy).then_inc(x1_hi, 1)
                    elif kind == "gu":
                        half, j = a
                        n = half * KB + j
                        act.wait_ge(gu_ready, b * (2 * KB) + n + 1)
                        need(act, ffn_full, b * (2 * KB) + n - 1)
                        if j == 0:
                            groups = (b + 1) * NG + 2 * half + 1
                            act.wait_ge(o_moved, (min(groups, B * NG) if isinstance(b, int) else groups) * 80)
                        nc.scalar.activation(th[:, j % 2], ring[:, BANKS[kind, off, a], 0:HALF], ACT.Tanh,
                                             scale=s1_c[:, j:j + 1]).then_inc(tanh_done, 1)
                    elif kind == "ffn_hi":
                        half, j = a
                        act.wait_ge(ffn_full, b * (2 * KB) + half * KB + j + 1)
                        need(act, f_ready, b * 2 + half)
                        nc.scalar.activation(Xhi[:, j], full_g[:, j % 2], ACT.Copy).then_inc(x_hi, 1)
                    elif kind == "table":
                        name, n = a
                        need(act, tables, b * TABLES + n)
                        nc.scalar.activation(loaded[:], ones_c[0:1],
                                             ACT.Exp if name == "Exp" else ACT.Gelu).then_inc(tables, 1)
                    elif kind == "h_act":
                        kind, half, j = a
                        u = u_of(kind, half, j)
                        act.wait_ge(h_ready, b * 32 + u + 1)
                        need(act, h_lo, b * 32 + u - 1)
                        src = ring[:, BANKS[kind, off, (half, j)], 0:HALF]
                        if kind == "h1":
                            hi, sc = Yhi[:, j], sh1_c[:, j:j + 1]
                        else:
                            hi, sc = Xhi[:, j], sh2_c[:, j:j + 1]
                        nc.scalar.activation(hi, src, ACT.Gelu, scale=sc)
                        nc.scalar.activation(full_h[:, u % 2], src, ACT.Gelu, scale=sc).then_inc(h_full, 1)

            pipeline(act, work)

        @block.vector
        def _(dve):
            nc.vector.memset(Osb[0:G * D], 0.0).then_inc(osb_set, 1)
            nc.vector.memset(Osb[G * D:P], 1.0).then_inc(osb_set, 1)
            nc.vector.memset(pO[:], 0.0)
            nc.vector.memset(ring[:], 0.0).then_inc(setup_v, 1)
            dve.wait_ge(params_in, 16 * N_PARAMS)
            dve.wait_ge(consts, N_CONSTS)
            nc.vector.tensor_copy(sel[:].rearrange("h c n -> h (c n)"), probs[0:2 * H, 0, 0, 0:C])
            nc.vector.tensor_scalar(s1_c, s1_c, 0.5, None, ALU.mult).then_inc(setup_v, 1)
            for c in range(CB):
                spread = nc.vector.tensor_scalar(full_g[:, c, 0:P], ident[:], 0.0, bv_c[:, c:c + 1], ALU.mult, ALU.add)
            spread.then_inc(setup_v, 1)
            dve.wait_ge(setup_v, 3)
            nc.vector.tensor_tensor(s2_c, s2_c, s1_c, ALU.mult)
            dve.wait_ge(setup_t, 1)
            nc.vector.tensor_tensor(b_tot[:], pM[:, 0, 0:C], b_tot[:], ALU.add).then_inc(setup_v, 1)

            tests = [(n, w, at) for n, w in enumerate(FFN) for at in range(0, w.shape[1] * w.shape[2], PIECE)]
            n_tests = len(tests)
            nc.vector.memset(low[:], 0).then_inc(setup_v, 1)

            def weight_test():
                n, w, at = tests.pop(0)
                dve.wait_ge(weights_in[n], 16 * (w.shape[1] * w.shape[2] // PIECE))
                dve.wait_ge(setup_v, 5 + n_tests - len(tests) - 1)
                words = w[:].bitcast(I32).rearrange("p k n -> p (k n)")[:, at:at + PIECE]
                nc.vector.scalar_tensor_tensor(out=low[:], in0=words, scalar=LOW_BITS, in1=low[:],
                                               op0=ALU.bitwise_and, op1=ALU.bitwise_or).then_inc(setup_v, 1)

            def weight_bits():
                while tests:
                    weight_test()
                dve.wait_ge(setup_v, 5 + n_tests)
                nc.vector.tensor_reduce(lowmax, low[:], AX_X, ALU.max).then_inc(setup_v, 1)
                dve.wait_ge(setup_t, 2)
                nc.vector.tensor_copy(flag[:], pM[0:1, 0, 0:1]).then_inc(setup_v, 1)

            def work(i, steps):
                for kind, off, a in steps:
                    b = i + off
                    if tests and i == 0 and (kind == "neg_max" and a[0] != 1 or kind == "max" and off == 1):
                        weight_test()
                    if kind == "max":
                        g, t, p = a
                        n = m_cols(t)
                        nth = b * HEADS + (g * TB + TB - 1 - t) * G + 2 * p
                        need(dve, nt_ready, b * NG + g)
                        for s in range(2):
                            dve.wait_ge(m_ready, nth + s + 1)
                            held(dve)
                            nc.vector.tensor_tensor_reduce(
                                pM[:, s, 0:n], pM[:, s, 0:n], mask[:, T - n:T], 1.0, NEG, ALU.add, ALU.max,
                                mx[:, t, 2 * p + s:2 * p + s + 1]).then_inc(m_done, 1)
                    elif kind == "neg_max":
                        g, = a
                        dve.wait_ge(nm_hi_done, b * NG + g + 1)
                        nc.vector.scalar_tensor_tensor(
                            out=nm[32:NM_ROWS], in0=ring[32:NM_ROWS, BANKS[kind, off, a]], scalar=-1.0,
                            in1=nm[32:NM_ROWS].bitcast(F32),
                            op0=ALU.mult, op1=ALU.subtract).then_inc(nm_lo_done, 1)
                    elif kind == "qk":
                        g, = a
                        dve.wait_ge(qk_hi, b * NG + g + 1)
                        nc.vector.scalar_tensor_tensor(
                            out=c_lo[:], in0=ring[:, BANKS[kind, off, a]], scalar=bqk_c[:, g:g + 1],
                            in1=c_hi[:].bitcast(F32), op0=ALU.add, op1=ALU.subtract).then_inc(qk_lo, 1)
                    elif kind == "x1_turn":
                        c, = a
                        dve.wait_ge(x1_hi, b * CB + c + 1)
                        nc.vector.tensor_tensor(x1Tlo[:, c], ring[:, BANKS[kind, off, a]], x1Thi[:, c].bitcast(F32),
                                                ALU.subtract).then_inc(x1_lo, 1)
                    elif kind == "gu":
                        half, j = a
                        n = b * (2 * KB) + half * KB + j
                        gate, up = (ring[:, BANKS[kind, off, a], m * HALF:(m + 1) * HALF] for m in range(2))
                        dve.wait_ge(tanh_done, n + 1)
                        nc.vector.scalar_tensor_tensor(out=th[:, j % 2], in0=th[:, j % 2], scalar=1.0, in1=up,
                                                       op0=ALU.add, op1=ALU.mult).then_inc(gated, 1)
                        dve.wait_ge(gated, n + 1)
                        need(dve, x_lo, n - 1)
                        nc.vector.scalar_tensor_tensor(out=full_g[:, j % 2], in0=gate,
                                                       scalar=s2_c[:, j:j + 1], in1=th[:, j % 2],
                                                       op0=ALU.mult, op1=ALU.mult).then_inc(ffn_full, 1)
                    elif kind == "h_rest":
                        layer, half, j = a
                        u = u_of(layer, half, j)
                        dve.wait_ge(h_full, b * 32 + u + 1)
                        hi, lo = (Yhi[:, j], Ylo[:, j]) if layer == "h1" else (Xhi[:, j], Xlo[:, j])
                        nc.vector.tensor_tensor(lo, full_h[:, u % 2], hi.bitcast(F32), ALU.subtract).then_inc(h_lo, 1)
                    elif kind == "rec_save":
                        dve.wait_ge(den_in, (b + 1) * 16)
                        need(dve, rec_saved, b * 16)
                        nc.vector.reciprocal(dn[:], dn[:]).then_inc(rc_done, 1)
                        dve.wait_ge(rc_done, b * 3 + 1)
                        nc.vector.tensor_copy(rc[:, 0], dn[:]).then_inc(rc_done, 1)
                        dve.wait_ge(rc_done, b * 3 + 2)
                        nc.vector.tensor_tensor(rc[:, 1], dn[:], rc[:, 0].bitcast(F32), ALU.subtract).then_inc(rc_done, 1)
                    elif kind == "den_turn":
                        for m in range(CB):
                            dve.wait_ge(r_ready, b * CB + m + 1)
                            nc.vector.tensor_tensor(Oc[:, m], Oc[:, m], ring[:, BANKS[kind, off, (m,)]],
                                                    ALU.mult).then_inc(o_norm, 1)
                    elif kind == "y":
                        half, = a
                        rows = xr[:, 2 * half:2 * half + 2]
                        dve.wait_ge(y_ready, b * 2 + half + 1)
                        dve.wait_ge(xr_ready, b + 1)
                        nc.vector.tensor_tensor(rows, ring[:, BANKS[kind, off, a]].rearrange("p (t c) -> p t c", c=C),
                                                rows, ALU.add).then_inc(ln1, 1)
                        dve.wait_ge(ln1, b * LN1 + 2 * half + 1)
                        for t in (2 * half, 2 * half + 1):
                            st = nc.vector.bn_stats(st1[:, t], xr[:, t])
                        st.then_inc(ln1, 1)
                    elif kind == "ln1_stats":
                        dve.wait_ge(ln1, b * LN1 + 4)
                        held(dve)
                        for t in range(TB):
                            mv = nc.vector.bn_aggr(mv1[:, t], st1[:, t])
                        mv.then_inc(ln1, 1)
                        dve.wait_ge(ln1, b * LN1 + 5)
                        nc.vector.tensor_scalar(rs1[:], mv1[:, :, 1], EPS, None, ALU.add).then_inc(ln1, 1)
                    elif kind == "ln1":
                        dve.wait_ge(ln1_pow, b + 1)
                        need(dve, xt_ready, b * CB)
                        need(dve, ln2, (b - 1) * LN2 + 8)
                        for t in range(TB):
                            row = nc.vector.tensor_scalar(x1[:, t], xr[:, t], mv1[:, t, 0:1], rs1[:, t:t + 1],
                                                          ALU.subtract, ALU.mult)
                        row.then_inc(ln1, 1)
                    elif kind == "ffn_out":
                        half, = a
                        at = b * LN2 + 6 * half
                        dve.wait_ge(f_ready, b * 2 + half + 1)
                        need(dve, stored, (b * 2 + half) * 16)
                        for t in range(2):
                            scaled = nc.vector.tensor_tensor(z[:, t], ring[:, BANKS[kind, off, a], t * C:(t + 1) * C],
                                                             s3b[:], ALU.mult)
                        scaled.then_inc(ln2, 1)
                        dve.wait_ge(ln2, at + 1)
                        nc.vector.tensor_tensor(z[:], z[:], x1[:, 2 * half:2 * half + 2], ALU.add).then_inc(ln2, 1)
                    elif kind == "ln2_stats":
                        half, = a
                        at = b * LN2 + 6 * half
                        dve.wait_ge(ln2, at + 2)
                        for t in range(2):
                            st = nc.vector.bn_stats(st2[:, t], z[:, t])
                        st.then_inc(ln2, 1)
                        dve.wait_ge(ln2, at + 3)
                        held(dve)
                        for t in range(2):
                            mv = nc.vector.bn_aggr(mv2[:, t], st2[:, t])
                        mv.then_inc(ln2, 1)
                        dve.wait_ge(ln2, at + 4)
                        nc.vector.tensor_scalar(rs2[:], mv2[:, :, 1], EPS, None, ALU.add).then_inc(ln2, 1)
                    elif kind == "ln2":
                        half, = a
                        dve.wait_ge(ln2_pow, b * 2 + half + 1)
                        for t in range(2):
                            row = nc.vector.tensor_scalar(z[:, t], z[:, t], mv2[:, t, 0:1], rs2[:, t:t + 1],
                                                          ALU.subtract, ALU.mult)
                        row.then_inc(ln2, 1)

            for i in (-1, 0, 1, 2):
                work(i, steps_of(i))
                if i == 0:
                    weight_bits()
            with dve.Fori(3, B - 1) as i:
                work(i, steps_of(None))
            for i in (B - 1, B, B + 1):
                work(i, steps_of(i))

        @block.tensor
        def _(pe):
            RELEASE = {
                "qk": lambda g: (qk_lo, NG, g + 1),
                "v": lambda kt: (v_copied, TB, kt + 1),
                "gu": lambda half, j: (ffn_full, 2 * KB, half * KB + j + 1),
                "h1": lambda half, j: (h_full, 32, u_of("h1", half, j) + 1),
                "h2": lambda half, j: (h_full, 32, u_of("h2", half, j) + 1),
                "ffn_out": lambda half: (ln2, LN2, 6 * half + 1),
                "y": lambda half: (ln1, LN1, 2 * half + 1),
                "x1_turn": lambda c: (x1_lo, CB, c + 1),
                "neg_max": lambda g: (nm_lo_done, NG, g + 1),
                "den_turn": lambda m: (o_norm, CB, m + 1),
            }

            def iteration(i, steps, taken, general):

                def bank(kind, off, a):
                    n = BANKS[kind, off, a]
                    if n in taken:
                        last, last_off, last_a = taken[n]
                        s, per, nth = RELEASE[last](*last_a)
                        pe.wait_ge(s, (i + last_off) * per + nth)
                    taken[n] = (kind, off, a)
                    return ring[:, n]

                def parts(w, act):
                    return (w.bitcast(F32), act.bitcast(F32)) if general else (w, act)

                for kind, off, a in steps:
                    b = i + off
                    if kind == "exp":
                        g, kt, p = a
                        n, slot = e_cols(kt), g % 2
                        if kt == 0 and p == 0:
                            pe.wait_ge(nm_in, (b * NG + g + 1) * 64)
                        for s in range(2):
                            need(pe, exp_done, b * HEADS + 2 * e_of(g, kt, p) + s - 1)
                            rows = slice(SROWS * s, SROWS * (s + 1))
                            nc.tensor.matmul(pS[:, s, 0:n], Ks[rows, slot, p, kt * P:(kt + 1) * P],
                                             Qs[rows, slot, p, kt * P:T], start=True, stop=True).then_inc(e_ready, 1)
                    elif kind == "max":
                        g, t, p = a
                        n, slot = m_cols(t), g % 2
                        nth = b * HEADS + (g * TB + TB - 1 - t) * G + 2 * p
                        if t == TB - 1 and p == 0:
                            pe.wait_ge(stack_in[slot], (b * 2 + g // 2 + 1) * 32)
                        for s in range(2):
                            need(pe, m_done, nth + s - 1)
                            rows = slice(SROWS * s, SROWS * (s + 1))
                            nc.tensor.matmul(pM[:, s, 0:n], Qs[rows, slot, p, t * P:(t + 1) * P],
                                             Ks[rows, slot, p, 0:n], start=True, stop=True).then_inc(m_ready, 1)
                    elif kind == "neg_max":
                        g, = a
                        pe.wait_ge(m_done, b * HEADS + (g + 1) * TB * G)
                        to = bank(kind, off, a)
                        for t in range(TB):
                            for at in (0, 32):
                                mm = nc.tensor.matmul(to[at:at + G, t * P:(t + 1) * P], mx[:, t], ident[:],
                                                      start=True, stop=True)
                        mm.then_inc(nt_ready, 1)
                    elif kind == "pv":
                        g, kt = a
                        n = e_cols(kt)
                        if kt == 0:
                            if g == 0:
                                pe.wait_ge(v_copied, (b + 1) * TB)
                            need(pe, o_out, b * NG + g)
                        pe.wait_ge(mask_done, b * (NG * TB * PAIRS) + e_of(g, kt, PAIRS - 1) + 1)
                        for p in range(PAIRS):
                            for s in range(2):
                                j = 2 * p + s
                                mm = nc.tensor.matmul(pO[32 * j:32 * j + VW, kt * P:T], Vo[:, kt, G * g + j],
                                                      probs[:, e_of(g, kt, p) % NP_BUF, s, 0:n],
                                                      start=(kt == 0), stop=(kt == TB - 1))
                        mm.then_inc(pv_done, 1)
                    elif kind == "qk":
                        g, = a
                        pe.wait_ge(xT_in, (b + 1) * 16)
                        to = bank(kind, off, a)
                        for c in range(CB):
                            mm = nc.tensor.matmul(to, Wqk[:, c, g], xTs[:, c], start=(c == 0), stop=(c == CB - 1))
                        mm.then_inc(qk_ready, 1)
                    elif kind == "v":
                        kt, = a
                        to = bank(kind, off, a)
                        for c in range(CB):
                            mm = nc.tensor.matmul(to[:, 0:C], xTs[:, c, kt * P:(kt + 1) * P], Wv[:, c],
                                                  start=(c == 0), stop=(c == CB - 1))
                        mm.then_inc(v_ready, 1)
                    elif kind == "den_turn":
                        pe.wait_ge(rec_in, (b + 1) * 16)
                        for m in range(CB):
                            to = bank(kind, off, (m,))
                            nc.tensor.matmul(to, sel[:, m], rec[:], start=True, stop=True).then_inc(r_ready, 1)
                    elif kind == "y":
                        half, = a
                        pe.wait_ge(o_norm, (b + 1) * CB)
                        to = bank(kind, off, a)
                        for t in range(2):
                            tok = slice((2 * half + t) * P, (2 * half + t + 1) * P)
                            for c in range(CB):
                                mm = nc.tensor.matmul(to[:, t * C:(t + 1) * C], Oc[:, c, tok], Wout[:, c],
                                                      start=(c == 0), stop=(c == CB - 1))
                        mm.then_inc(y_ready, 1)
                    elif kind == "x1_turn":
                        c, = a
                        pe.wait_ge(ln1, (b + 1) * LN1)
                        to = bank(kind, off, a)
                        for t in range(TB):
                            mm = nc.tensor.transpose(to[:, t * P:(t + 1) * P], x1[:, t, c * P:(c + 1) * P], ident[:])
                        mm.then_inc(xt_ready, 1)
                    elif kind == "gu":
                        half, j = a
                        pe.wait_ge(x1_lo, (b + 1) * CB)
                        tok = slice(half * HALF, (half + 1) * HALF)
                        to = bank(kind, off, a)
                        for n, W in enumerate((W1, W2)):
                            for c in range(CB):
                                for X in (x1Thi, x1Tlo):
                                    w, x_part = parts(W[:, c, j * P:(j + 1) * P], X[:, c, tok])
                                    mm = nc.tensor.matmul(to[:, n * HALF:(n + 1) * HALF], w, x_part,
                                                          start=(c == 0 and X is x1Thi),
                                                          stop=(c == CB - 1 and X is x1Tlo))
                        mm.then_inc(gu_ready, 1)
                    elif kind in ("h1", "h2"):
                        half, j = a
                        W, src = (H1, (Xhi, Xlo)) if kind == "h1" else (H2, (Yhi, Ylo))
                        s, n = (x_lo, b * (2 * KB) + (half + 1) * KB) if kind == "h1" else (h_lo, b * 32 + half * 16 + KB)
                        to = bank(kind, off, a)[:, 0:HALF]
                        for k in range(KB):
                            if j == 0 and k in (0, KB - 1):
                                pe.wait_ge(s, n - (k == 0))
                            for m, X in enumerate(src):
                                w, x_part = parts(W[:, k, j * P:(j + 1) * P], X[:, k])
                                mm = nc.tensor.matmul(to, w, x_part, start=(k == 0 and m == 0),
                                                      stop=(k == KB - 1 and m == 1))
                        mm.then_inc(h_ready, 1)
                    elif kind == "ffn_out":
                        half, = a
                        to = bank(kind, off, a)
                        for t in range(2):
                            tok = slice(t * P, (t + 1) * P)
                            for k in range(KB):
                                if t == 0 and k in (0, KB - 1):
                                    pe.wait_ge(h_lo, b * 32 + half * 16 + 2 * KB - (k == 0))
                                for m, X in enumerate((Xhi, Xlo)):
                                    w, x_part = parts(W3[:, k], X[:, k, tok])
                                    mm = nc.tensor.matmul(to[:, t * C:(t + 1) * C], x_part, w,
                                                          start=(k == 0 and m == 0), stop=(k == KB - 1 and m == 1))
                        mm.then_inc(f_ready, 1)
                for n, (kind, off, a) in taken.items():
                    taken[n] = (kind, off - 1, a)

            def ffn_iterations(taken, general):
                for i in (1, 2):
                    iteration(i, steps_of(i), taken, general)
                with pe.Fori(3, B - 1) as i:
                    iteration(i, steps_of(None), taken, general)
                for i in (B - 1, B, B + 1):
                    iteration(i, steps_of(i), taken, general)

            pe.wait_ge(params_in, 16 * N_PARAMS)
            pe.wait_ge(setup_v, 3)
            for c in range(CB):
                mm = nc.tensor.matmul(pM[:, 0, 0:C], full_g[:, c, 0:P], Wout[:, c], start=(c == 0), stop=(c == CB - 1))
            mm.then_inc(setup_t, 1)
            pe.wait_ge(setup_v, 4)
            taken = {}
            for i in (-1, 0):
                iteration(i, steps_of(i), taken, False)
            chunks = sum(w.shape[1] * w.shape[2] // PIECE for w in FFN)
            pe.wait_ge(setup_v, 5 + chunks + 1)
            nc.tensor.matmul(pM[0:1, 0, 0:1], lowmax, ones_c, start=True, stop=True).then_inc(setup_t, 1)
            pe.wait_ge(setup_v, 5 + chunks + 2)
            has_low_bits = pe.value_load(flag[0:1, 0:1], min_val=0, max_val=1 << 20)
            with pe.If(has_low_bits > 0):
                ffn_iterations(dict(taken), True)
            with pe.Else():
                ffn_iterations(dict(taken), False)


def kernel(**inputs):
    import concourse.bacc as bacc
    from concourse.bass_utils import run_bass_kernel_spmd

    a = {k: np.asarray(v) for k, v in inputs.items()}
    x = a["L0_attn_x"]
    w_qkv, b_qkv = a["L0_attn_Wqkv"], a["L0_attn_bqkv"]
    w_qk = np.ascontiguousarray(w_qkv[:, :2 * C].reshape(C, 2, NG, G * D).transpose(0, 2, 1, 3)).reshape(C, NG, P)
    b_qk = b_qkv[:2 * C].reshape(2, NG, G * D).transpose(1, 0, 2).reshape(NG, P)
    cols = np.zeros((P, 40), np.float32)
    cols[:, 0:4] = b_qk.T
    cols[:, 4:6] = b_qkv[2 * C:].reshape(CB, P).T
    for n, name in enumerate(("w1_s", "w2_s", "h1_s", "h2_s")):
        cols[:, 8 * n + 8:8 * n + 16] = a["L0_ffn_" + name].reshape(KB, P).T
    arrays = {
        "x": np.ascontiguousarray(x),
        "xT": np.ascontiguousarray(x.transpose(0, 2, 1)),
        "w_qk": w_qk,
        "w_v": np.ascontiguousarray(w_qkv[:, 2 * C:]),
        "w_out": np.ascontiguousarray(a["L0_attn_Wout"]),
    }
    for name in ("w1", "w2", "h1", "h2", "w3"):
        arrays[name] = np.ascontiguousarray(a[f"L0_ffn_{name}_w"].T)
    arrays["cols"] = cols
    arrays["b_out"] = np.ascontiguousarray(a["L0_attn_bout"])
    arrays["s3"] = np.ascontiguousarray(a["L0_ffn_w3_s"])

    nc = bacc.Bacc("TRN2", target_bir_lowering=False, num_devices=1)
    args = {n: nc.dram_tensor(f"in_{n}", v.shape, F32, kind="ExternalInput").ap() for n, v in arrays.items()}
    out = nc.dram_tensor("out_0", (B, T, C), F32, kind="ExternalOutput").ap()
    build(nc, args["x"], args["xT"], args["w_qk"], args["w_v"], args["w_out"],
          [args[n] for n in ("w1", "w2", "h1", "h2", "w3")], args["cols"], args["b_out"], args["s3"], out)
    got = run_bass_kernel_spmd(nc, [{f"in_{n}": v for n, v in arrays.items()}], core_ids=[0])
    return got.results[0]["out_0"]
```
